# Optimizing a Trainium2 kernel written in Bass

```python
import numpy as np
import jax
import jax.numpy as jnp

def _softmax(x, axis=-1):
    return jax.nn.softmax(x, axis=axis)

def _gelu(x):
    return jax.nn.gelu(x, approximate=True)

def _silu(x):
    return jax.nn.silu(x)

def _sigmoid(x):
    return jax.nn.sigmoid(x)

def _layernorm(x, axis=-1, eps=1e-05):
    m = jnp.mean(x, axis=axis, keepdims=True)
    v = jnp.var(x, axis=axis, keepdims=True)
    return (x - m) / jnp.sqrt(v + eps)

def _scatter_add(tgt, idx, src, axis=0):
    return tgt.at[idx].add(src)

def _segment_sum(src, seg, n):
    return jax.ops.segment_sum(src, seg, n)
kernel_name = 'mk_hybrid_d1_jaxref_r4_eea4aa'

def setup_inputs(seed: int=0):
    np.random.seed(seed)
    _w = jnp.asarray

    def _L0_attn_a_setup():
        import jax, jax.numpy as jnp
        import numpy as np
        from math import sqrt
        N_HEAD = 16
        W_SCALE = 0.02

        def _reference_tuple_inner(x, W_dq, W_uq, W_dkv, W_uk, W_uv, W_o):
            B, T, C = x.shape
            nh = N_HEAD
            hs = C // nh
            n_kvl = W_dkv.shape[0]
            k_eff = (W_dq.T @ W_uq.T @ W_uk).reshape(nh, hs, n_kvl)
            v_eff = jnp.transpose((W_uv.T @ W_o.T).reshape(n_kvl, nh, hs), (1, 0, 2))
            c_kv = x @ W_dkv.T
            q = x @ W_dq.T @ W_uq.T
            q = q.reshape(B, T, nh, hs)
            q_lat = jnp.einsum('bqhd,hdl->bhql', q, k_eff)
            attn = jnp.einsum('bhql,bkl->bhqk', q_lat, c_kv) / sqrt(hs)
            causal = jnp.tril(jnp.ones((T, T), dtype=bool))
            attn = jnp.where(causal[None, None], attn, -jnp.inf)
            attn = jax.nn.softmax(attn, axis=-1)
            y_lat = jnp.einsum('bhqk,bkl->bhql', attn, c_kv)
            y = jnp.einsum('bhql,hld->bqhd', y_lat, v_eff).reshape(B, T, C)
            return (y, c_kv)
        key = jax.random.key(seed)
        ks = jax.random.split(key, 7)
        B, T, C = (2, 512, 256)
        QL, KVL = (128, 128)
        return {'x': jax.random.normal(ks[0], (B, T, C), dtype=jnp.float32), 'W_dq': jax.random.normal(ks[1], (QL, C), dtype=jnp.float32) * W_SCALE, 'W_uq': jax.random.normal(ks[2], (C, QL), dtype=jnp.float32) * W_SCALE, 'W_dkv': jax.random.normal(ks[3], (KVL, C), dtype=jnp.float32) * W_SCALE, 'W_uk': jax.random.normal(ks[4], (C, KVL), dtype=jnp.float32) * W_SCALE, 'W_uv': jax.random.normal(ks[5], (C, KVL), dtype=jnp.float32) * W_SCALE, 'W_o': jax.random.normal(ks[6], (C, C), dtype=jnp.float32) * W_SCALE}
    _L0_attn_a_in = _L0_attn_a_setup()

    def _L0_attn_b_setup():
        import jax, jax.numpy as jnp
        import numpy as np
        from jax.scipy.linalg import solve_triangular
        H = 4
        CHUNK = 64
        NORM_EPS = 1e-05

        def _l2norm(x):
            return x / jnp.clip(jnp.linalg.norm(x, axis=-1, keepdims=True), 1e-12)

        def _deltanet_forward(hidden_states, conv_w, Wq, Wk, Wv, Wb, Wg, norm_w, Wo):
            B, L, D = hidden_states.shape
            Kc = conv_w.shape[1]
            dqh = Wq.shape[1] // H
            dvh = Wv.shape[1] // H
            xp = jnp.pad(hidden_states, ((0, 0), (Kc - 1, 0), (0, 0)))
            h = sum((conv_w[:, i] * xp[:, i:i + L, :] for i in range(Kc)))
            h = jax.nn.silu(h)
            q = (h @ Wq).reshape(B, L, H, dqh).transpose(0, 2, 1, 3)
            k = (h @ Wk).reshape(B, L, H, dqh).transpose(0, 2, 1, 3)
            v = (h @ Wv).reshape(B, L, H, dvh).transpose(0, 2, 1, 3)
            q = _l2norm(q)
            k = _l2norm(k)
            beta = jax.nn.sigmoid(h @ Wb).transpose(0, 2, 1)
            qm = q.reshape(B * H, L, dqh)
            km = k.reshape(B * H, L, dqh)
            vm = v.reshape(B * H, L, dvh)
            bm = beta.reshape(B * H, L)
            Nc = L // CHUNK
            eye = jnp.eye(CHUNK, dtype=q.dtype)

            def per_head(qh, kh, vh, bh):
                qs = qh.reshape(Nc, CHUNK, dqh)
                ks_ = kh.reshape(Nc, CHUNK, dqh)
                vs = vh.reshape(Nc, CHUNK, dvh)
                bs = bh.reshape(Nc, CHUNK)

                def step(S, xs):
                    qc, kc, vc, bc = xs
                    kb = kc * bc[:, None]
                    A = jnp.tril(kb @ kc.T, -1)
                    U = solve_triangular(eye + A, vc * bc[:, None] - kb @ S, lower=True)
                    o = qc @ S + jnp.tril(qc @ kc.T) @ U
                    return (S + kc.T @ U, o)
                S0 = jnp.zeros((dqh, dvh), qh.dtype)
                _, o = jax.lax.scan(step, S0, (qs, ks_, vs, bs))
                return o.reshape(L, dvh)
            o = jax.vmap(per_head)(qm, km, vm, bm)
            o = o.reshape(B, H, L, dvh).transpose(0, 2, 1, 3)
            g = (h @ Wg).reshape(B, L, H, dvh)
            rms = o * jax.lax.rsqrt(jnp.mean(o * o, axis=-1, keepdims=True) + NORM_EPS)
            out = rms * norm_w * (g * jax.nn.sigmoid(g))
            return out.reshape(B, L, H * dvh) @ Wo
        key = jax.random.key(seed)
        ks = jax.random.split(key, 9)
        B, L, D = (4, 1024, 256)
        dk, dv = (128, 256)
        s = 0.02
        return {'hidden_states': jax.random.normal(ks[0], (B, L, D), jnp.float32), 'conv_w': jax.random.normal(ks[1], (D, 4), jnp.float32) * 0.2, 'Wq': jax.random.normal(ks[2], (D, dk), jnp.float32) * s, 'Wk': jax.random.normal(ks[3], (D, dk), jnp.float32) * s, 'Wv': jax.random.normal(ks[4], (D, dv), jnp.float32) * s, 'Wb': jax.random.normal(ks[5], (D, H), jnp.float32) * s, 'Wg': jax.random.normal(ks[6], (D, dv), jnp.float32) * s, 'norm_w': jnp.ones((dv // H,), jnp.float32), 'Wo': jax.random.normal(ks[7], (dv, D), jnp.float32) * s}
    _L0_attn_b_in = _L0_attn_b_setup()

    def _L0_ffn_setup():
        import jax, jax.numpy as jnp
        import numpy as np
        from jax import lax
        T, B, I, M, O = (64, 64, 256, 256, 256)

        def _xavier(key, shape):
            fan_out, fan_in = shape
            limit = float(np.sqrt(6.0 / (fan_in + fan_out)))
            return jax.random.uniform(key, shape, jnp.float32, -limit, limit)
        key = jax.random.key(seed)
        ks = jax.random.split(key, 9)
        x = jax.random.normal(ks[0], (T, B, I), jnp.float32)
        return {'x': x, 'wf': _xavier(ks[1], (M, I)), 'uf': _xavier(ks[2], (M, M)), 'bf': jnp.zeros((M,), jnp.float32), 'wi': _xavier(ks[3], (M, I)), 'ui': _xavier(ks[4], (M, M)), 'bi': jnp.zeros((M,), jnp.float32), 'wc': _xavier(ks[5], (M, I)), 'uc': _xavier(ks[6], (M, M)), 'bc': jnp.zeros((M,), jnp.float32), 'wo': _xavier(ks[7], (O, I)), 'uo': _xavier(ks[8], (O, M)), 'bo': jnp.zeros((O,), jnp.float32), 'in_c': jnp.zeros((M,), jnp.float32)}
    _L0_ffn_in = _L0_ffn_setup()
    _d = {'L0_attn_a_x': _L0_attn_a_in['x'], 'L0_attn_a_W_dq': _L0_attn_a_in['W_dq'], 'L0_attn_a_W_uq': _L0_attn_a_in['W_uq'], 'L0_attn_a_W_dkv': _L0_attn_a_in['W_dkv'], 'L0_attn_a_W_uk': _L0_attn_a_in['W_uk'], 'L0_attn_a_W_uv': _L0_attn_a_in['W_uv'], 'L0_attn_a_W_o': _L0_attn_a_in['W_o'], 'L0_attn_b_conv_w': _L0_attn_b_in['conv_w'], 'L0_attn_b_Wq': _L0_attn_b_in['Wq'], 'L0_attn_b_Wk': _L0_attn_b_in['Wk'], 'L0_attn_b_Wv': _L0_attn_b_in['Wv'], 'L0_attn_b_Wb': _L0_attn_b_in['Wb'], 'L0_attn_b_Wg': _L0_attn_b_in['Wg'], 'L0_attn_b_norm_w': _L0_attn_b_in['norm_w'], 'L0_attn_b_Wo': _L0_attn_b_in['Wo'], 'L0_ffn_wf': _L0_ffn_in['wf'], 'L0_ffn_uf': _L0_ffn_in['uf'], 'L0_ffn_bf': _L0_ffn_in['bf'], 'L0_ffn_wi': _L0_ffn_in['wi'], 'L0_ffn_ui': _L0_ffn_in['ui'], 'L0_ffn_bi': _L0_ffn_in['bi'], 'L0_ffn_wc': _L0_ffn_in['wc'], 'L0_ffn_uc': _L0_ffn_in['uc'], 'L0_ffn_bc': _L0_ffn_in['bc'], 'L0_ffn_wo': _L0_ffn_in['wo'], 'L0_ffn_uo': _L0_ffn_in['uo'], 'L0_ffn_bo': _L0_ffn_in['bo'], 'L0_ffn_in_c': _L0_ffn_in['in_c']}
    _x0 = _d['L0_attn_a_x']
    _d['L0_attn_a_x'] = jax.random.normal(jax.random.fold_in(jax.random.key(seed), 1), (4, 1024, 256), dtype=_x0.dtype)
    del _x0
    return _d

def reference(L0_attn_a_x, L0_attn_a_W_dq, L0_attn_a_W_uq, L0_attn_a_W_dkv, L0_attn_a_W_uk, L0_attn_a_W_uv, L0_attn_a_W_o, L0_attn_b_conv_w, L0_attn_b_Wq, L0_attn_b_Wk, L0_attn_b_Wv, L0_attn_b_Wb, L0_attn_b_Wg, L0_attn_b_norm_w, L0_attn_b_Wo, L0_ffn_wf, L0_ffn_uf, L0_ffn_bf, L0_ffn_wi, L0_ffn_ui, L0_ffn_bi, L0_ffn_wc, L0_ffn_uc, L0_ffn_bc, L0_ffn_wo, L0_ffn_uo, L0_ffn_bo, L0_ffn_in_c):

    def _L0_attn_a_ref(x, W_dq, W_uq, W_dkv, W_uk, W_uv, W_o):
        import jax, jax.numpy as jnp
        import numpy as np
        from math import sqrt
        N_HEAD = 16
        W_SCALE = 0.02

        def _reference_tuple_inner(x, W_dq, W_uq, W_dkv, W_uk, W_uv, W_o):
            B, T, C = x.shape
            nh = N_HEAD
            hs = C // nh
            n_kvl = W_dkv.shape[0]
            k_eff = (W_dq.T @ W_uq.T @ W_uk).reshape(nh, hs, n_kvl)
            v_eff = jnp.transpose((W_uv.T @ W_o.T).reshape(n_kvl, nh, hs), (1, 0, 2))
            c_kv = x @ W_dkv.T
            q = x @ W_dq.T @ W_uq.T
            q = q.reshape(B, T, nh, hs)
            q_lat = jnp.einsum('bqhd,hdl->bhql', q, k_eff)
            attn = jnp.einsum('bhql,bkl->bhqk', q_lat, c_kv) / sqrt(hs)
            causal = jnp.tril(jnp.ones((T, T), dtype=bool))
            attn = jnp.where(causal[None, None], attn, -jnp.inf)
            attn = jax.nn.softmax(attn, axis=-1)
            y_lat = jnp.einsum('bhqk,bkl->bhql', attn, c_kv)
            y = jnp.einsum('bhql,hld->bqhd', y_lat, v_eff).reshape(B, T, C)
            return (y, c_kv)
        return _reference_tuple_inner(x, W_dq, W_uq, W_dkv, W_uk, W_uv, W_o)[0]

    def _L0_attn_b_ref(hidden_states, conv_w, Wq, Wk, Wv, Wb, Wg, norm_w, Wo):
        import jax, jax.numpy as jnp
        import numpy as np
        from jax.scipy.linalg import solve_triangular
        H = 4
        CHUNK = 64
        NORM_EPS = 1e-05

        def _l2norm(x):
            return x / jnp.clip(jnp.linalg.norm(x, axis=-1, keepdims=True), 1e-12)

        def _deltanet_forward(hidden_states, conv_w, Wq, Wk, Wv, Wb, Wg, norm_w, Wo):
            B, L, D = hidden_states.shape
            Kc = conv_w.shape[1]
            dqh = Wq.shape[1] // H
            dvh = Wv.shape[1] // H
            xp = jnp.pad(hidden_states, ((0, 0), (Kc - 1, 0), (0, 0)))
            h = sum((conv_w[:, i] * xp[:, i:i + L, :] for i in range(Kc)))
            h = jax.nn.silu(h)
            q = (h @ Wq).reshape(B, L, H, dqh).transpose(0, 2, 1, 3)
            k = (h @ Wk).reshape(B, L, H, dqh).transpose(0, 2, 1, 3)
            v = (h @ Wv).reshape(B, L, H, dvh).transpose(0, 2, 1, 3)
            q = _l2norm(q)
            k = _l2norm(k)
            beta = jax.nn.sigmoid(h @ Wb).transpose(0, 2, 1)
            qm = q.reshape(B * H, L, dqh)
            km = k.reshape(B * H, L, dqh)
            vm = v.reshape(B * H, L, dvh)
            bm = beta.reshape(B * H, L)
            Nc = L // CHUNK
            eye = jnp.eye(CHUNK, dtype=q.dtype)

            def per_head(qh, kh, vh, bh):
                qs = qh.reshape(Nc, CHUNK, dqh)
                ks_ = kh.reshape(Nc, CHUNK, dqh)
                vs = vh.reshape(Nc, CHUNK, dvh)
                bs = bh.reshape(Nc, CHUNK)

                def step(S, xs):
                    qc, kc, vc, bc = xs
                    kb = kc * bc[:, None]
                    A = jnp.tril(kb @ kc.T, -1)
                    U = solve_triangular(eye + A, vc * bc[:, None] - kb @ S, lower=True)
                    o = qc @ S + jnp.tril(qc @ kc.T) @ U
                    return (S + kc.T @ U, o)
                S0 = jnp.zeros((dqh, dvh), qh.dtype)
                _, o = jax.lax.scan(step, S0, (qs, ks_, vs, bs))
                return o.reshape(L, dvh)
            o = jax.vmap(per_head)(qm, km, vm, bm)
            o = o.reshape(B, H, L, dvh).transpose(0, 2, 1, 3)
            g = (h @ Wg).reshape(B, L, H, dvh)
            rms = o * jax.lax.rsqrt(jnp.mean(o * o, axis=-1, keepdims=True) + NORM_EPS)
            out = rms * norm_w * (g * jax.nn.sigmoid(g))
            return out.reshape(B, L, H * dvh) @ Wo
        return _deltanet_forward(hidden_states, conv_w, Wq, Wk, Wv, Wb, Wg, norm_w, Wo)

    def _L0_ffn_ref(x, wf, uf, bf, wi, ui, bi, wc, uc, bc, wo, uo, bo, in_c):
        import jax, jax.numpy as jnp
        import numpy as np
        from jax import lax
        T, B, I, M, O = (64, 64, 256, 256, 256)

        def _xavier(key, shape):
            fan_out, fan_in = shape
            limit = float(np.sqrt(6.0 / (fan_in + fan_out)))
            return jax.random.uniform(key, shape, jnp.float32, -limit, limit)
        batch = x.shape[1]
        c0 = jnp.broadcast_to(in_c, (batch, in_c.shape[0]))

        def step(c, xt):
            ft = jax.nn.sigmoid(xt @ wf.T + c @ uf.T + bf)
            it = jax.nn.sigmoid(xt @ wi.T + c @ ui.T + bi)
            gt = jnp.tanh(xt @ wc.T + c @ uc.T + bc)
            c = ft * c + it * gt
            return (c, None)
        c_final, _ = lax.scan(step, c0, x)
        h = jnp.tanh(jnp.einsum('tbi,oi->tbo', x, wo) + c_final @ uo.T + bo)
        return h
    x = L0_attn_a_x
    x = x + _L0_attn_a_ref(_layernorm(x, axis=-1), L0_attn_a_W_dq, L0_attn_a_W_uq, L0_attn_a_W_dkv, L0_attn_a_W_uk, L0_attn_a_W_uv, L0_attn_a_W_o)
    x = x + _L0_ffn_ref(_layernorm(x, axis=-1), L0_ffn_wf, L0_ffn_uf, L0_ffn_bf, L0_ffn_wi, L0_ffn_ui, L0_ffn_bi, L0_ffn_wc, L0_ffn_uc, L0_ffn_bc, L0_ffn_wo, L0_ffn_uo, L0_ffn_bo, L0_ffn_in_c)
    x = x + _L0_attn_b_ref(_layernorm(x, axis=-1), L0_attn_b_conv_w, L0_attn_b_Wq, L0_attn_b_Wk, L0_attn_b_Wv, L0_attn_b_Wb, L0_attn_b_Wg, L0_attn_b_norm_w, L0_attn_b_Wo)
    x = x + _L0_ffn_ref(_layernorm(x, axis=-1), L0_ffn_wf, L0_ffn_uf, L0_ffn_bf, L0_ffn_wi, L0_ffn_ui, L0_ffn_bi, L0_ffn_wc, L0_ffn_uc, L0_ffn_bc, L0_ffn_wo, L0_ffn_uo, L0_ffn_bo, L0_ffn_in_c)
    return x

_drawn_inputs = setup_inputs


def setup_inputs(seed=0):
    import zlib

    import numpy as np

    out = dict(_drawn_inputs(seed))
    spreads = {'L0_attn_b_norm_w': (1.0, 0.6),
     'L0_ffn_bf': (0.0, 2.0),
     'L0_ffn_bi': (0.0, 2.0),
     'L0_ffn_bc': (0.0, 0.8),
     'L0_ffn_bo': (0.0, 0.708),
     'L0_ffn_in_c': (0.0, 1.994)}
    factors = {'L0_attn_a_W_dq': 8.0,
     'L0_attn_a_W_uq': 8.0,
     'L0_attn_a_W_dkv': 8.0,
     'L0_attn_a_W_uk': 8.0,
     'L0_attn_a_W_uv': 8.0,
     'L0_attn_a_W_o': 8.0,
     'L0_attn_b_conv_w': 5.66,
     'L0_attn_b_Wq': 5.704,
     'L0_attn_b_Wk': 5.7,
     'L0_attn_b_Wv': 5.719,
     'L0_attn_b_Wb': 8.0,
     'L0_attn_b_Wg': 5.688,
     'L0_attn_b_Wo': 5.962,
     'L0_ffn_wf': 4.641,
     'L0_ffn_uf': 8.0,
     'L0_ffn_wi': 2.982,
     'L0_ffn_ui': 6.606}
    for name, (base, spread) in spreads.items():
        noise = np.random.default_rng([zlib.crc32(name.encode()), seed]).standard_normal(out[name].shape)
        drawn = base * np.exp(spread * noise) if base else spread * noise
        out[name] = jnp.asarray(drawn.astype(out[name].dtype))
    for name, factor in factors.items():
        out[name] = (out[name] * factor).astype(out[name].dtype)
    return out
```

```python
from contextlib import ExitStack

import numpy as np

import concourse.bass as bass
from concourse import mybir

F32 = mybir.dt.float32
BF16 = mybir.dt.bfloat16
ALU = mybir.AluOpType
ACT = mybir.ActivationFunctionType
AXIS_X = mybir.AxisListType.X

P = 128
B, T, C = 4, 1024, 256
TOKENS = B * T
TILES = TOKENS // P
KT = C // P
BANK = 512
GROUPS = TOKENS // BANK
TPG = BANK // P
EPS = 1e-5

NH, HS = 16, 16
HPU = 4
UNITS_PER_B = NH // HPU
QB = T // P
QC = T // BANK
SPLIT_Q = (0, 1, 0, 1, 2, 0)
SPLIT_K = (0, 0, 1, 1, 0, 2)
PRODUCTS = len(SPLIT_Q)
SCORE_ROWS = PRODUCTS * HS
MAX_ROWS = 3
STACKS = 3
MAX_LEAD = 8
MASKED = -float(2.0 ** 100)

DH, DK, DV = 4, 32, 64
CH = 32
CHUNKS = T // CH
SOLVE = P // (B * DH)
WINDOW = 2 * SOLVE

ENGINES = ("sync", "gpsimd", "tensor", "scalar", "vector")


class Step:

    def __init__(self, engine, emit, after, arrival=None):
        self.engine, self.emit, self.after, self.arrival = engine, emit, after, arrival
        self.signals, self.count = False, 0


class Program:

    def __init__(self, nc, ctx):
        self.nc, self.ctx = nc, ctx
        self.queue = {e: [] for e in ENGINES}
        self.done = {e: ctx.enter_context(nc.semaphore(f"{e}_done")) for e in ENGINES}
        self.arrivals = []

    def step(self, engine, emit, after=()):
        s = Step(engine, emit, [])
        self._wait_for(s, after)
        self.queue[engine].append(s)
        return s

    def _wait_for(self, s, after):
        for a in after:
            if a is None:
                continue
            if isinstance(a, (list, tuple)):
                self._wait_for(s, a)
                continue
            if a.arrival is None:
                a.signals = True
            s.after.append(a)

    def arrival(self, name):
        a = [self.ctx.enter_context(self.nc.semaphore(name)), 0]
        self.arrivals.append(a)
        return a

    def dma(self, engine, out, in_, arrival, after=()):
        arrival[1] += 16
        s = Step(engine, lambda e: e.dma_start(out, in_), [], (arrival[0], arrival[1]))
        self._wait_for(s, after)
        self.queue[engine].append(s)
        return s

    def tail(self):
        return [q[-1] for q in self.queue.values() if q]

    def run(self):
        for e in ENGINES:
            n = 0
            for s in self.queue[e]:
                if s.arrival is None and s.signals:
                    n += 1
                    s.count = n
        block = self.ctx.enter_context(self.nc.Block())
        enter = {"sync": block.sync, "gpsimd": block.gpsimd, "tensor": block.tensor, "scalar": block.scalar,
                 "vector": block.vector}
        for e in ENGINES:
            def body(eng, e=e):
                seen = {}
                for s in self.queue[e]:
                    for a in s.after:
                        sem, value, key = (self.done[a.engine], a.count, a.engine) if a.arrival is None else \
                            (a.arrival[0], a.arrival[1], id(a.arrival[0]))
                        if seen.get(key, 0) < value:
                            eng.wait_ge(sem, value)
                            seen[key] = value
                    ins = s.emit(eng)
                    if s.arrival is not None:
                        ins.then_inc(s.arrival[0], 16)
                    elif s.signals:
                        ins.then_inc(self.done[e], 1)
                if e == "sync":
                    for sem, total in self.arrivals:
                        if total:
                            eng.wait_ge(sem, total)
            enter[e](body)


class Slot:

    def __init__(self, buf):
        self.buf, self.free = buf, []


class Ring:
    def __init__(self, bufs):
        self.slots, self.at = [Slot(b) for b in bufs], -1

    def next(self):
        self.at = (self.at + 1) % len(self.slots)
        return self.slots[self.at]


class Kernel:
    def __init__(self, nc, ctx, io):
        self.nc, self.ctx, self.io = nc, ctx, io
        self.p = Program(nc, ctx)
        self.psum_pairs = [ctx.enter_context(nc.psum_tensor(f"psum{i}", [P, 2, BANK], F32)) for i in range(4)]
        self.bank = [Slot(pair[:, j, :]) for pair in self.psum_pairs for j in range(2)]

    def pe(self, emit, after=()):
        return self.p.step("tensor", emit, after)

    def act(self, out, in_, func=ACT.Copy, after=(), **kw):
        return self.p.step("scalar", lambda e: e.activation(out, in_, func, **kw), after)

    def tt(self, out, a, b, op, after=(), on="vector"):
        return self.p.step(on, lambda e: e.tensor_tensor(out, a, b, op), after)

    def ts(self, out, a, s1, s2, op0, op1=ALU.bypass, after=(), on="vector"):
        return self.p.step(on, lambda e: e.tensor_scalar(out, a, s1, s2, op0, op1), after)

    def copy(self, out, in_, after=(), on="vector"):
        if on == "scalar":
            return self.act(out, in_, after=after)
        return self.p.step(on, lambda e: e.tensor_copy(out, in_), after)

    def reduce(self, out, in_, op, negate=False, after=()):
        return self.p.step("vector", lambda e: e.tensor_reduce(out, in_, AXIS_X, op, negate=negate), after)

    def memset(self, out, value, on="gpsimd", after=()):
        return self.p.step(on, lambda e: e.memset(out, value), after)

    def matmuls(self, parts, after=(), lint=True):
        def emit(e):
            for out, lhsT, rhs, start, stop in parts:
                last = e.matmul(out, lhsT, rhs, start=start, stop=stop, skip_group_check=not lint)
            return last
        return self.pe(emit, after)

    def transposes(self, parts, after=()):
        def emit(e):
            for out, in_, ident in parts:
                last = e.transpose(out, in_, ident)
            return last
        return self.pe(emit, after)


def allocate(k):
    nc, ctx = k.nc, k.ctx

    def sb(name, shape, dt=F32):
        return ctx.enter_context(nc.sbuf_tensor(name, shape, dt))

    k.xr = sb("residual", [P, TILES, C])
    k.ident = sb("identity", [P, P])
    k.mask_scores = sb("mask_scores", [P, P])
    k.mask_a = sb("mask_strict", [P, CH])
    k.mask_attn = sb("mask_incl", [P, CH])
    k.mask_quad = sb("mask_quadrant", [P, 4])
    k.ident16 = sb("identity16", [P, P], BF16)
    k.mask16 = sb("mask_scores16", [P, P], BF16)
    k.half_power = sb("minus_half", [P, P])
    k.stats = sb("ln_stats", [P, TILES, 6])
    k.moments = sb("ln_moments", [P, TILES, 2])
    k.rstd = sb("ln_rstd", [P, TILES])
    k.xn = Ring([sb(f"normed{i}", [P, TPG, C]) for i in range(2)])


def load_constants(k):
    p, io = k.p, k.io
    arrival = p.arrival("constants_in")
    at = 0
    for buf in (k.ident, k.mask_scores, k.mask_a, k.mask_attn, k.mask_quad):
        n = buf.shape[1]
        last = p.dma("scalar", buf[:, :], io["constants"][:, at:at + n], arrival)
        at += n
    k.constants = last
    a = k.copy(k.ident16[:, :], k.ident[:, :], [last])
    b = k.copy(k.mask16[:, :], k.mask_scores[:, :], [last])
    k.const16 = [a, b]
    k.powers = k.memset(k.half_power[:, :], -0.5)


def layernorm(k, tiles, ready):
    slot = k.xn.next()
    g = slice(tiles[0], tiles[-1] + 1, tiles[1] - tiles[0])
    out = []
    for i in tiles:
        s = k.p.step("vector", lambda e, i=i: e.bn_stats(k.stats[:, i, :], k.xr[:, i, :]), [ready[i]])
        m = k.p.step("vector", lambda e, i=i: e.bn_aggr(k.moments[:, i, :], k.stats[:, i, :]), [s])
    a = k.ts(k.rstd[:, g], k.moments[:, g, 1], EPS, None, ALU.add, after=[m], on="gpsimd")
    r = k.tt(k.rstd[:, g], k.rstd[:, g], k.half_power[:, 0:len(tiles)], ALU.pow, after=[a, k.powers], on="gpsimd")
    for j, i in enumerate(tiles):
        out.append(k.ts(slot.buf[:, j, :], k.xr[:, i, :], k.moments[:, i, 0:1], k.rstd[:, i:i + 1],
                        ALU.subtract, ALU.mult, after=[r, slot.free]))
    return slot, out


def layernorm_transposed(k, tiles, ready, banks, write):
    slot, normed = layernorm(k, tiles, ready)
    evacuated = []
    for kt in range(KT):
        bank = banks[kt % len(banks)]
        turned = k.transposes([(bank.buf[:, j * P:(j + 1) * P], slot.buf[:, j, kt * P:(kt + 1) * P], k.ident[:, :])
                               for j in range(TPG)], [normed, bank.free, k.constants])
        done = write(kt, bank.buf, [turned])
        bank.free = [done]
        evacuated.append(done)
    slot.free = [turned]
    return evacuated


def attention(k):
    with ExitStack() as ctx:
        v_rows = ctx.enter_context(k.nc.sbuf_tensor("v_rows", [P, TILES, NH, HS + 1], F32))
        with ExitStack() as inner:
            parts_written, v_done = attention_project(k, inner, v_rows)
        attention_scores(k, ctx, v_rows, parts_written, v_done)


def load_x(k):
    k.ready = {}
    for g in range(GROUPS):
        a = k.p.arrival(f"x_in{g}")
        s = k.p.dma("sync", k.xr[:, g * TPG:(g + 1) * TPG, :],
                    k.io["x"][g * BANK:(g + 1) * BANK, :].rearrange("(i p) c -> p i c", p=P), a)
        for i in range(TPG):
            k.ready[g * TPG + i] = s


def attention_project(k, ctx, v_rows):
    nc, p, io = k.nc, k.p, k.io

    def sb(name, shape, dt=F32):
        return ctx.enter_context(nc.sbuf_tensor(name, shape, dt))

    w = {}
    arrived = {}
    for name, shape in (("wdqT", [P, KT, P]), ("wdkvT", [P, KT, P]), ("wuqT", [P, C]), ("wuq", [P, KT, P]),
                        ("wuk", [P, KT, P]), ("wdq", [P, C]), ("wuv", [P, KT, P]), ("woT", [P, KT, C])):
        w[name] = sb("a_" + name, shape)
        arrival = p.arrival(f"in_{name}")
        dst = w[name][:, :, :] if len(shape) == 3 else w[name][:, :]
        src = io[name]
        arrived[name] = p.dma("scalar", dst, src.rearrange("(a p) n -> p a n", p=P) if len(shape) == 3 else src, arrival)
    xT = Ring([sb(f"a_xT{i}", [P, KT, BANK]) for i in range(2)])
    lat = Ring([sb(f"a_latent{i}", [P, 2, BANK]) for i in range(2)])
    rest = Ring([sb(f"a_rest{i}", [P, BANK]) for i in range(4)])
    parts = Ring([sb(f"a_parts{i}", [P, 3, BANK], BF16) for i in range(4)])
    sent = [p.arrival(f"parts_out{i}") for i in range(4)]
    keff = sb("a_keffT", [P, C])
    veff = sb("a_veff", [P, C])
    wuk_q = sb("a_wuk_q", [P, P])

    ring = Ring([])
    ring.slots = k.bank[2:8]
    b0 = ring.next()
    t1 = k.matmuls([(b0.buf[:, 0:P], w["wuq"][:, kt, :], w["wuk"][:, kt, :], kt == 0, kt == KT - 1) for kt in range(KT)],
                   [arrived["wuq"], arrived["wuk"]])
    t1c = k.copy(wuk_q[:, :], b0.buf[:, 0:P], [t1])
    b0.free = [t1c]
    b1 = ring.next()
    ke = k.matmuls([(b1.buf[:, 0:C], wuk_q[:, :], w["wdq"][:, :], True, True)], [t1c, arrived["wdq"]])
    kec = k.copy(keff[:, :], b1.buf[:, 0:C], [ke])
    b1.free = [kec]
    b2 = ring.next()
    ve = k.matmuls([(b2.buf[:, 0:C], w["wuv"][:, kt, :], w["woT"][:, kt, :], kt == 0, kt == KT - 1) for kt in range(KT)],
                   [arrived["wuv"], arrived["woT"]])
    vec = k.copy(veff[:, :], b2.buf[:, 0:C], [ve])
    b2.free = [vec]
    ones = k.memset(v_rows[:, :, :, HS:HS + 1], 1.0)

    load_x(k)
    x_in = k.ready
    written = {}
    v_done = []
    for g in range(GROUPS):
        cols = slice(g * BANK, (g + 1) * BANK)
        xs = xT.next()
        evac = layernorm_transposed(
            k, list(range(g * TPG, (g + 1) * TPG)), x_in, k.bank[0:2],
            lambda kt, bank, after: k.copy(xs.buf[:, kt, :], bank[:, :], after + xs.free, on="vector"))
        ls = lat.next()
        lat_done = []
        for n, name in enumerate(("wdqT", "wdkvT")):
            bk = ring.next()
            m = k.matmuls([(bk.buf[:, :], w[name][:, kt, :], xs.buf[:, kt, :], kt == 0, kt == KT - 1) for kt in range(KT)],
                          [evac, bk.free, arrived[name]])
            e = k.copy(ls.buf[:, n, :], bk.buf[:, :], [m, ls.free], on="scalar")
            bk.free = [e]
            lat_done.append(e)
        xs.free = [m]
        readers = []
        for which, (weight, ready) in enumerate((("q", arrived["wuqT"]), ("k", kec))):
            for mt in range(KT):
                lhsT = w["wuqT"][:, mt * P:(mt + 1) * P] if weight == "q" else keff[:, mt * P:(mt + 1) * P]
                bk = ring.next()
                m = k.matmuls([(bk.buf[:, :], lhsT, ls.buf[:, which, :], True, True)], [lat_done[which], bk.free, ready])
                readers.append(m)
                ps, rs = parts.next(), rest.next()
                hi = k.copy(ps.buf[:, 0, :], bk.buf[:, :], [m, ps.free], on="scalar")
                r = k.tt(rs.buf[:, :], bk.buf[:, :], ps.buf[:, 0, :], ALU.subtract, [hi, rs.free])
                bk.free = [r]
                mid = k.copy(ps.buf[:, 1, :], rs.buf[:, :], [r], on="gpsimd")
                lo = k.tt(ps.buf[:, 2, :], rs.buf[:, :], ps.buf[:, 1, :], ALU.subtract, [mid], on="gpsimd")
                rs.free = [lo]
                d = p.dma("sync", io["parts"][which, :, mt * P:(mt + 1) * P, cols].rearrange("s c t -> c s t"),
                          ps.buf[:, :, :], sent[parts.at], [lo])
                ps.free = [d]
                written.setdefault(g // QC, []).append(d)
        for j in range(0, TPG, 2):
            bk = ring.next()
            m = k.matmuls([(bk.buf[:, n * C:(n + 1) * C], ls.buf[:, 1, (j + n) * P:(j + n + 1) * P], veff[:, :], True, True)
                           for n in range(2)], [lat_done[1], vec, bk.free])
            i = g * TPG + j
            e = k.copy(v_rows[:, i:i + 2, :, 0:HS], bk.buf[:, :].rearrange("p (i h d) -> p i h d", i=2, h=NH), [m],
                       on="scalar")
            bk.free = [e]
            v_done.append(e)
        ls.free = readers + [m]
    return written, v_done + [ones]


def attention_scores(k, ctx, v_rows, parts_written, v_done):
    nc, p, io = k.nc, k.p, k.io
    before = p.tail()

    def sb(name, shape, dt=F32):
        return ctx.enter_context(nc.sbuf_tensor(name, shape, dt))

    qst = [sb(f"q_stack{i}", [P, HPU, T], BF16) for i in range(STACKS)]
    kst = [sb(f"k_stack{i}", [P, HPU, T], BF16) for i in range(STACKS)]
    weights = [sb(f"weights{i}", [P, HPU, BANK]) for i in range(2)]
    maxima = [sb(f"maxima{i}", [P, HPU, QB, 2]) for i in range(2)]
    negmax = [sb(f"negmax{i}", [P, HPU * QB]) for i in range(2)]
    mparts = [sb(f"max_parts{i}", [HPU * QB, MAX_ROWS, P], BF16) for i in range(2)]
    mrest = [sb(f"max_rest{i}", [HPU * QB, P]) for i in range(2)]
    oT = Ring([sb(f"att_oT{i}", [P, BANK]) for i in range(2)])
    rden = Ring([sb(f"att_rden{i}", [P, TPG, HPU]) for i in range(2)])
    onorm = Ring([sb(f"att_o{i}", [P, TPG, HPU, HS]) for i in range(2)])
    st_banks = [k.bank[0:2], k.bank[2:4]]
    max_ring = Ring([])
    max_ring.slots = k.bank[4:6]
    o_bank, misc = k.bank[6], k.bank[7]

    st_free = [[b.free for b in k.bank[0:2]], [b.free for b in k.bank[2:4]]]
    zero = k.memset(o_bank.buf[:, :], 0.0, on="vector", after=[o_bank.free, before])
    o_bank.free = [zero]
    arrived_stack = [p.arrival(f"stack_in{i}") for i in range(STACKS)]
    arrived_max = [p.arrival(f"max_in{i}") for i in range(STACKS)]
    ones = [k.memset(kst[s][SCORE_ROWS:SCORE_ROWS + MAX_ROWS, :, :], 1.0, on="vector", after=[before])
            for s in range(STACKS)]

    units = [(b, g) for b in range(B) for g in range(UNITS_PER_B)]
    stack_done, max_done, stack_free = {}, {}, {}
    readers = {}

    def load(u):
        b, g = units[u]
        s = u % STACKS
        for n in range(PRODUCTS):
            for which, dst, part in ((0, qst[s], SPLIT_Q[n]), (1, kst[s], SPLIT_K[n])):
                src = io["parts"][which, part, g * HPU * HS:(g + 1) * HPU * HS, b * T:(b + 1) * T]
                d = p.dma("sync", dst[n * HS:(n + 1) * HS, :, :], src.rearrange("(h d) t -> d h t", h=HPU),
                          arrived_stack[s], [before, parts_written[b], stack_free.get(u - STACKS)])
        stack_done[u] = d

    per_unit = [(h, qb, c * BANK, min(BANK, (qb + 1) * P - c * BANK)) for qb in range(QB) for h in range(HPU)
                for c in range((qb + 1) * P // BANK + ((qb + 1) * P % BANK > 0))]
    max_tiles = [(u, *t) for u in range(len(units)) for t in per_unit]
    state = {"at": 0}
    reduced = {}

    def max_tile():
        if state["at"] == len(max_tiles):
            return
        u, h, qb, k0, w = max_tiles[state["at"]]
        first = state["at"] % len(per_unit) == 0
        state["at"] += 1
        s = u % STACKS
        if first:
            reduced[u] = []
        bk = max_ring.next()
        lhsT = qst[s][0:SCORE_ROWS, h, qb * P:(qb + 1) * P]
        diagonal = k0 + w == (qb + 1) * P
        mm = [(bk.buf[:, 0:w], lhsT, kst[s][0:SCORE_ROWS, h, k0:k0 + w], True, not diagonal)]
        if diagonal:
            mm.append((bk.buf[:, w - P:w], k.ident16[:, :], k.mask16[:, :], False, True))
        m = k.matmuls(mm, [stack_done[u], bk.free, k.const16])
        r = k.reduce(maxima[u % 2][:, h, qb, k0 // BANK:k0 // BANK + 1], bk.buf[:, 0:w], ALU.max, negate=True,
                     after=[m, readers.get(("max", u - 2))])
        bk.free = [r]
        reduced[u].append(r)
        if len(reduced[u]) == len(per_unit):
            finish_max(u)

    def finish_max(u):
        n, s = u % 2, u % STACKS
        half = QB // 2
        nm = negmax[n][:, :].rearrange("p (h q) -> p h q", h=HPU)
        free = readers.get(("max", u - 2), [])
        a = k.copy(nm[:, :, 0:half], maxima[n][:, :, 0:half, 0], [reduced[u], free])
        c = k.tt(nm[:, :, half:QB], maxima[n][:, :, half:QB, 0], maxima[n][:, :, half:QB, 1], ALU.min, [reduced[u], free])
        rows = misc.buf[0:HPU * QB, 0:P]
        t = k.transposes([(rows, negmax[n][:, :], k.ident[:, :])], [a, c, misc.free])
        hi = k.copy(mparts[n][:, 0, :], rows, [t, readers.get(("mparts", u - 2))])
        r = k.tt(mrest[n][:, :], rows, mparts[n][:, 0, :], ALU.subtract, [hi])
        misc.free = [r]
        mid = k.copy(mparts[n][:, 1, :], mrest[n][:, :], [r])
        lo = k.tt(mparts[n][:, 2, :], mrest[n][:, :], mparts[n][:, 1, :], ALU.subtract, [mid])
        for j in range(MAX_ROWS):
            dst = qst[s][SCORE_ROWS + j:SCORE_ROWS + j + 1, :, :].rearrange("o h (q t) -> o (h q) t", q=QB)
            d = p.dma("gpsimd", dst, mparts[n][:, j, :], arrived_max[s], [lo, stack_free.get(u - STACKS)])
        max_done[u] = d
        readers[("max", u)] = [t, a, c]
        readers[("mparts", u)] = [d]

    exp_done = {}
    w_free = [[], []]
    o_state = {"free": o_bank.free}

    def score_pair(u, step, kb, qc, pair):
        s = u % STACKS
        q0 = max(qc * BANK, kb * P)
        w = (qc + 1) * BANK - q0
        mm = []
        for j in range(2):
            h = 2 * pair + j
            diagonal = kb * P >= qc * BANK
            out = st_banks[pair][j].buf
            mm.append((out[:, 0:w], kst[s][0:SCORE_ROWS + MAX_ROWS, h, kb * P:(kb + 1) * P],
                       qst[s][0:SCORE_ROWS + MAX_ROWS, h, q0:q0 + w], True, not diagonal))
            if diagonal:
                mm.append((out[:, 0:P], k.mask16[:, :], k.ident16[:, :], False, True))
        m = k.matmuls(mm, [stack_done[u], max_done[u], ones[s], st_free[pair], k.const16])
        last_scores[u] = m
        slot = step % 2
        src = st_pair[pair][:, :, 0:w]
        e = k.act(weights[slot][:, 2 * pair:2 * pair + 2, 0:w], src, ACT.Exp, [m, w_free[slot], before], scale=HS ** -0.5)
        st_free[pair] = [e]
        return e, w, q0 - qc * BANK

    last_scores = {}
    first_out = [True]

    def values(u, step, kb, qc, exps, w, off):
        b, _ = units[u]
        g = units[u][1]
        slot = step % 2
        last_kb = kb == (qc + 1) * TPG - 1
        mm = [(o_bank.buf[32 * h:32 * h + HS + 1, off:off + w], v_rows[:, b * QB + kb, g * HPU + h, :],
               weights[slot][:, h, 0:w], kb == 0, last_kb) for h in range(HPU)]
        m = k.matmuls(mm, [exps, v_done, o_state["free"] if kb == 0 else None])
        w_free[slot] = [m]
        if last_kb:
            os_ = oT.next()
            e = k.copy(os_.buf[:, :], o_bank.buf[:, :], [m, os_.free], on="scalar")
            o_state["free"] = [e]
            return (u, qc, os_, e)

    updated = {}

    def output(u, qc, os_, e):
        b, g = units[u]
        t = k.transposes([(misc.buf[:, j * P:(j + 1) * P], os_.buf[:, j * P:(j + 1) * P], k.ident[:, :])
                          for j in range(TPG)], [e, misc.free])
        os_.free = [t]
        rows = misc.buf[:, :].rearrange("p (i h d) -> p i h d", i=TPG, h=HPU)
        rs, ns = rden.next(), onorm.next()
        r = k.p.step("vector", lambda en: en.reciprocal(rs.buf[:, :, :], rows[:, :, :, HS]), [t, rs.free])
        mul = k.tt(ns.buf[:, :, :, :], rows[:, :, :, 0:HS],
                   rs.buf[:, :, :].rearrange("p i (h o) -> p i h o", o=1).to_broadcast([P, TPG, HPU, HS]),
                   ALU.mult, [r, ns.free])
        misc.free = [mul]
        rs.free = [mul]
        i = b * QB + qc * TPG
        x = k.xr[:, i:i + TPG, g * HPU * HS:(g + 1) * HPU * HS]
        a = k.tt(x, x, ns.buf[:, :, :, :].rearrange("p i h d -> p i (h d)"), ALU.add, [mul, before], on="gpsimd")
        ns.free = [a]
        for j in range(TPG):
            updated[i + j] = a

    st_pair = [k.psum_pairs[0], k.psum_pairs[1]]
    for u in range(min(STACKS, len(units))):
        load(u)
    lead = len(per_unit) + MAX_LEAD
    for _ in range(lead):
        max_tile()
    steps = [(u, kb, qc) for u in range(len(units)) for qc in range(QC) for kb in range((qc + 1) * TPG)]
    per_step = len(per_unit) // (len(steps) // len(units))
    pending, finishing = None, None
    for n, (u, kb, qc) in enumerate(steps):
        new_unit = n % (len(steps) // len(units)) == 0
        e0, w, off = score_pair(u, n, kb, qc, 0)
        for _ in range(per_step // 2):
            max_tile()
        e1, w, off = score_pair(u, n, kb, qc, 1)
        if finishing:
            output(*finishing)
            finishing = None
        if pending:
            finishing = values(*pending)
            if new_unit:
                done = u - 1
                stack_free[done] = [last_scores[done]]
                if done + STACKS < len(units):
                    load(done + STACKS)
        pending = (u, n, kb, qc, [e0, e1], w, off)
        for _ in range(per_step - per_step // 2):
            max_tile()
    if finishing:
        output(*finishing)
    output(*values(*pending))
    o_bank.free = o_state["free"]
    for n in range(2):
        for j in range(2):
            k.bank[2 * n + j].free = st_free[n]
    k.ready = updated


def ffn(k):
    nc, p, io = k.nc, k.p, k.io
    before = p.tail()
    tag = f"f{len(p.arrivals)}_"
    with ExitStack() as ctx:
        def sb(name, shape, dt=F32):
            return ctx.enter_context(nc.sbuf_tensor(tag + name, shape, dt))

        wts = sb("weights", [P, 8, KT, C])
        bias = sb("biases", [P, 4, KT])
        bias0 = sb("first_biases", [P, 3, KT])
        bo = sb("bo", [P, C])
        a_w, a_b = p.arrival(tag + "w_in"), p.arrival(tag + "b_in")
        w_in = p.dma("sync", wts[:, :, :, :], io["ffn_w"], a_w, [before])
        p.dma("sync", bias[:, :, :], io["ffn_b"], a_b, [before])
        b_in = p.dma("sync", bo[:, :], io["ffn_bo"].to_broadcast([P, C]), a_b, [before])
        init = bias[:, 3, :]
        xT = sb("xT", [P, KT, TOKENS])
        gates = Ring([sb(f"gates{i}", [P, 3, KT, BANK]) for i in range(2)])
        state = [Ring([sb(f"state{j}_{i}", [P, KT, BANK]) for i in range(2)]) for j in range(QC)]
        cu = [sb(f"state_out{j}", [P, TPG, C]) for j in range(QC)]
        hid = Ring([sb(f"hidden{i}", [P, 2, C]) for i in range(3)])

        ln_banks = k.bank[0:2]
        ring = Ring([])
        ring.slots = k.bank[2:8]

        bk = ring.next()
        m = k.matmuls([(bk.buf[:, 2 * g + mt:2 * g + mt + 1], wts[:, 4 + g, kt, mt * P:(mt + 1) * P], init[:, kt:kt + 1],
                        kt == 0, kt == KT - 1) for g in range(3) for mt in range(KT) for kt in range(KT)],
                      [w_in, b_in, bk.free])
        first_bias = k.tt(bias0[:, :, :], bk.buf[:, 0:6].rearrange("p (g m) -> p g m", g=3), bias[:, 0:3, :], ALU.add,
                          [m, before])
        bk.free = [first_bias]

        normed = {}

        def norm(g):
            cols = slice(g * BANK, (g + 1) * BANK)
            normed[g] = layernorm_transposed(
                k, list(range(g * TPG, (g + 1) * TPG)), k.ready, ln_banks,
                lambda kt, bank, after: k.copy(xT[:, kt, cols], bank[:, :], after + [before], on="vector"))

        current = [None] * QC

        def recur(t, j):
            g0 = (t * QC + j) * BANK
            gs = gates.next()
            parts = []
            for gate, func in ((0, ACT.Sigmoid), (1, ACT.Sigmoid), (2, ACT.Tanh)):
                for mt in range(KT):
                    bk = ring.next()
                    ms = slice(mt * P, (mt + 1) * P)
                    mm = [(bk.buf[:, :], wts[:, gate, kt, ms], xT[:, kt, g0:g0 + BANK], kt == 0, t == 0 and kt == KT - 1)
                          for kt in range(KT)]
                    m = k.matmuls(mm, [normed[t * QC + j], w_in, bk.free])
                    if t:
                        c, written = current[j]
                        m = k.matmuls([(bk.buf[:, :], wts[:, 4 + gate, kt, ms], c.buf[:, kt, :], False, kt == KT - 1)
                                       for kt in range(KT)], [written])
                    b = (bias if t else bias0)[:, gate, mt:mt + 1]
                    a = k.act(gs.buf[:, gate, mt, :], bk.buf[:, :], func, [m, first_bias, gs.free, before], bias=b)
                    bk.free = [a]
                    parts.append(a)
            new = state[j].next()
            kept = []
            if t:
                kept.append(k.tt(gs.buf[:, 0, :, :], gs.buf[:, 0, :, :], current[j][0].buf[:, :, :], ALU.mult, [parts]))
                current[j][0].free = [m, kept[-1]]
            else:
                for mt in range(KT):
                    kept.append(k.ts(gs.buf[:, 0, mt, :], gs.buf[:, 0, mt, :], init[:, mt:mt + 1], None, ALU.mult,
                                     after=[parts, b_in]))
            fresh = k.tt(gs.buf[:, 1, :, :], gs.buf[:, 1, :, :], gs.buf[:, 2, :, :], ALU.mult, [parts], on="gpsimd")
            w = k.tt(new.buf[:, :, :], gs.buf[:, 0, :, :], gs.buf[:, 1, :, :], ALU.add, [kept, fresh, new.free, before])
            gs.free = [w]
            current[j] = (new, [w])

        updated = {}

        def state_output(j):
            c, written = current[j]
            done = []
            for half in range(2):
                bk = ring.next()
                m = k.matmuls([(bk.buf[:, n * C:(n + 1) * C], c.buf[:, kt, (2 * half + n) * P:(2 * half + n + 1) * P],
                                wts[:, 7, kt, :], kt == 0, kt == KT - 1) for n in range(2) for kt in range(KT)],
                              [written, bk.free])
                a = k.tt(cu[j][:, 2 * half:2 * half + 2, :], bk.buf[:, :].rearrange("p (n c) -> p n c", n=2),
                         bo[:, :].rearrange("p (o c) -> p o c", o=1).to_broadcast([P, 2, C]), ALU.add, [m, b_in, before])
                bk.free = [a]
                done.append(a)
            return done

        def hidden(t, j, half, cu_done):
            bk, hs = ring.next(), hid.next()
            i = (t * QC + j) * TPG + 2 * half
            m = k.matmuls([(bk.buf[:, n * C:(n + 1) * C], xT[:, kt, (i + n) * P:(i + n + 1) * P], wts[:, 3, kt, :],
                            kt == 0, kt == KT - 1) for n in range(2) for kt in range(KT)], [normed[t * QC + j], bk.free])
            s = k.tt(hs.buf[:, :, :], bk.buf[:, :].rearrange("p (n c) -> p n c", n=2), cu[j][:, 2 * half:2 * half + 2, :],
                     ALU.add, [m, cu_done, hs.free, before])
            bk.free = [s]
            h = k.act(hs.buf[:, :, :], hs.buf[:, :, :], ACT.Tanh, [s])
            x = k.xr[:, i:i + 2, :]
            a = k.tt(x, x, hs.buf[:, :, :], ALU.add, [h], on="gpsimd")
            hs.free = [a]
            updated[i] = updated[i + 1] = a

        norm(0)
        norm(1)
        for t in range(B):
            for j in range(QC):
                recur(t, j)
                if (t + 1) * QC + j < GROUPS:
                    norm((t + 1) * QC + j)
        for j in range(QC):
            cu_done = state_output(j)
            for half in range(2):
                for t in range(B):
                    hidden(t, j, half, cu_done)
        k.ready = updated


def delta(k):
    nc, p, io = k.nc, k.p, k.io
    before = p.tail()
    with ExitStack() as ctx:
        def sb(name, shape, dt=F32):
            return ctx.enter_context(nc.sbuf_tensor("d_" + name, shape, dt))

        def ring(name, n, shape):
            return Ring([sb(f"{name}{i}", shape) for i in range(n)])

        NQ = 2 * DH * DK
        QK = DH * DK
        HV = DH * DV
        w_qkb = sb("w_qkb", [P, KT, NQ + DH])
        w_vg = sb("w_vg", [P, KT, 2 * HV])
        w_o = sb("w_o", [P, KT, C])
        conv = sb("conv", [P, KT, 4])
        norm_w = sb("norm_w", [P, DV])
        a_w = p.arrival("delta_w_in")
        for dst, src in ((w_qkb[:, :, :], io["d_qkb"]), (w_vg[:, :, :], io["d_vg"]), (w_o[:, :, :], io["d_wo"]),
                         (conv[:, :, :], io["d_conv"]), (norm_w[:, :], io["d_norm"].to_broadcast([P, DV]))):
            w_in = p.dma("sync", dst, src, a_w, [before])

        TAPS = 4
        xg = ring("xT", 2, [P, KT, B, TAPS - 1 + P])
        acc = ring("conv_sum", 2, [P, B * P])
        sig = ring("conv_sig", 2, [P, B * P])
        hT = ring("hT", 2, [P, KT, TPG, B, CH])
        qk = ring("qk_rows", 2, [P, NQ])
        sq = ring("squares", 2, [P, NQ])
        ss = ring("sumsq", 4, [P, 2 * DH])
        qn = ring("q_normed", 2, [P, QK])
        kb = ring("k_beta", 2, [P, QK])
        beta = ring("beta", 4, [P, DH])
        kq_bd = ring("kT_quads", 2, [P, DH, P])
        attn = ring("attn", 2, [P, DH, CH])
        a_rows = sb("a_rows", [P, SOLVE, DH, CH])
        kn = ring("k_normed", WINDOW, [P, QK])
        qkT = ring("q_kb_T", WINDOW, [P, 2, P])
        attnT = ring("attnT", WINDOW, [P, DH, CH])
        bv = ring("beta_v", WINDOW, [P, HV])
        gate = ring("gate", WINDOW, [P, HV])
        sys_a = ring("systems", 1, [P, CH, CH])
        inv = ring("inverse", 1, [P, CH, CH])
        prod = ring("products", 1, [P, CH, CH])
        invT = ring("inv_quads", 2, [P, DH, P])
        attn_bd = ring("attn_quads", 2, [P, DH, P])
        s_bd = sb("state_quads", [P, B, DH, DV])
        rhs = ring("rhs", 2, [P, HV])
        u_rows = ring("u_rows", 2, [P, HV])
        u_bd = sb("u_quads", [P, DH, B, DV])
        osq = ring("o_squares", 2, [P, HV])
        oss = ring("o_sumsq", 2, [P, DH])
        on = ring("o_normed", 2, [P, HV])
        oT = ring("oT", 2, [P, KT, B, TPG, CH])

        zeroed = [k.memset(s_bd[:, :, :, :], 0.0, on="gpsimd", after=[before]),
                  k.memset(u_bd[:, :, :, :], 0.0, on="gpsimd", after=[before])]
        for s in invT.slots:
            s.free = [k.memset(s.buf[:, :, :], 0.0, on="gpsimd", after=[before])]
        first_pad = k.memset(xg.slots[0].buf[:, :, :, 0:TAPS - 1], 0.0, on="gpsimd", after=[before])
        ln_bank, qk_bank, vg_bank, turn_bank, prod_bank, chain_bank, s_bank, o_bank = k.bank
        a_out = p.arrival("systems_out")
        a_in = p.arrival("systems_in")
        inv_out = p.arrival("inverses_out")
        inv_in = [p.arrival(f"inverse_in{i}") for i in range(2)]

        kept = {}
        solved = {}
        state = {"pad": first_pad, "a_free": [], "systems": None}

        def bcast(ap, n, at):
            return ap.rearrange("p (x o) -> p x o", o=1).to_broadcast([P, at, n])

        def prepare_group(G):
            xs = xg.next()
            tiles = [b * QB + G for b in range(B)]
            prev = xg.slots[(xg.at - 1) % 2]
            if G:
                pad = k.copy(xs.buf[:, :, :, 0:TAPS - 1], prev.buf[:, :, :, P:P + TAPS - 1], [state["x_ready"], xs.free],
                             on="gpsimd")
            else:
                pad = state["pad"]
            evac = layernorm_transposed(
                k, tiles, k.ready, [ln_bank],
                lambda kt, bank, after: k.act(xs.buf[:, kt, :, TAPS - 1:TAPS - 1 + P],
                                              bank[:, :].rearrange("p (b t) -> p b t", b=B),
                                              after=after + xs.free + before))
            state["x_ready"] = evac
            yield
            hs = hT.next()
            h_done = []
            for kt in range(KT):
                ac, sg = acc.next(), sig.next()
                a3 = ac.buf[:, :].rearrange("p (b t) -> p b t", b=B)
                s = k.ts(a3, xs.buf[:, kt, :, 0:P], conv[:, kt, 0:1], None, ALU.mult,
                         after=[evac, pad, w_in, ac.free, before])
                for i in range(1, TAPS):
                    s = p.step("vector", lambda e, i=i, a3=a3, kt=kt: e.scalar_tensor_tensor(
                        out=a3, in0=xs.buf[:, kt, :, i:i + P], scalar=conv[:, kt, i:i + 1], in1=a3,
                        op0=ALU.mult, op1=ALU.add), [s])
                    if i == 2:
                        yield
                g = k.act(sg.buf[:, :], ac.buf[:, :], ACT.Sigmoid, [s, sg.free, before])
                m = k.tt(hs.buf[:, kt, :, :, :].rearrange("p c b t -> p b c t"),
                         ac.buf[:, :].rearrange("p (b c t) -> p b c t", b=B, c=TPG),
                         sg.buf[:, :].rearrange("p (b c t) -> p b c t", b=B, c=TPG), ALU.mult, [g, hs.free, before],
                         on="gpsimd")
                ac.free = sg.free = [m]
                h_done.append(m)
                yield
            xs.free = [s] + ([pad] if G else [])
            state["pad_reader"] = s
            last = None
            for c in range(TPG):
                yield from prepare_chunk(G * TPG + c, hs, c, h_done)
            hs.free = [kept[G * TPG + TPG - 1]["h_read"]]

        def prepare_chunk(ch, hs, c, h_done):
            cols = [hs.buf[:, kt, c, :, :].rearrange("p b t -> p (b t)") for kt in range(KT)]
            ps = qk_bank.buf
            m = k.matmuls([(ps[:, 0:NQ + DH], cols[kt], w_qkb[:, kt, :], kt == 0, kt == KT - 1) for kt in range(KT)],
                          [h_done, w_in, qk_bank.free])
            be, rows, sqs, sss = beta.next(), qk.next(), sq.next(), ss.next()
            b = k.act(be.buf[:, :], ps[:, NQ:NQ + DH], ACT.Sigmoid, [m, be.free, before])
            e = k.act(rows.buf[:, :], ps[:, 0:NQ], after=[m, rows.free, before])
            qk_bank.free = [b, e]
            q2 = k.tt(sqs.buf[:, :], rows.buf[:, :], rows.buf[:, :], ALU.mult, [e, sqs.free, before], on="gpsimd")
            r = k.reduce(sss.buf[:, :], sqs.buf[:, :].rearrange("p (h d) -> p h d", d=DK), ALU.add,
                         after=[q2, sss.free, before])
            sqs.free = [r]
            mx = k.ts(sss.buf[:, :], sss.buf[:, :], 1e-24, None, ALU.max, after=[r], on="gpsimd")
            rn = k.tt(sss.buf[:, :], sss.buf[:, :], k.half_power[:, 0:2 * DH], ALU.pow, [mx], on="gpsimd")
            yield
            vg = vg_bank.buf
            mv = k.matmuls([(vg[:, :], cols[kt], w_vg[:, kt, :], kt == 0, kt == KT - 1) for kt in range(KT)],
                           [h_done, w_in, vg_bank.free])
            qs, ks, kbs = qn.next(), kn.next(), kb.next()
            nq = k.tt(qs.buf[:, :].rearrange("p (h d) -> p h d", d=DK), rows.buf[:, 0:QK].rearrange("p (h d) -> p h d", d=DK),
                      bcast(sss.buf[:, 0:DH], DK, DH), ALU.mult, [rn, e, qs.free, before], on="gpsimd")
            nk = k.tt(ks.buf[:, :].rearrange("p (h d) -> p h d", d=DK), rows.buf[:, QK:NQ].rearrange("p (h d) -> p h d", d=DK),
                      bcast(sss.buf[:, DH:2 * DH], DK, DH), ALU.mult, [rn, e, ks.free, before], on="gpsimd")
            nb = k.tt(kbs.buf[:, :].rearrange("p (h d) -> p h d", d=DK), ks.buf[:, :].rearrange("p (h d) -> p h d", d=DK),
                      bcast(be.buf[:, :], DK, DH), ALU.mult, [nk, b, kbs.free, before], on="gpsimd")
            rows.free = [nk]
            sss.free = [nk]
            bvs, gts = bv.next(), gate.next()
            sgm = k.act(gts.buf[:, :], vg[:, HV:2 * HV], ACT.Sigmoid, [mv, gts.free, before])
            v = k.tt(bvs.buf[:, :].rearrange("p (h d) -> p h d", d=DV), vg[:, 0:HV].rearrange("p (h d) -> p h d", d=DV),
                     bcast(be.buf[:, :], DV, DH), ALU.mult, [sgm, b, bvs.free, before])
            be.free = [v, nb]
            g1 = k.tt(gts.buf[:, :], vg[:, HV:2 * HV], gts.buf[:, :], ALU.mult, [sgm])
            vg_bank.free = [v, g1]
            g2 = k.tt(gts.buf[:, :].rearrange("p (h d) -> p h d", d=DV), gts.buf[:, :].rearrange("p (h d) -> p h d", d=DV),
                      norm_w[:, :].rearrange("p (o d) -> p o d", o=1).to_broadcast([P, DH, DV]), ALU.mult, [g1, w_in],
                      on="gpsimd")
            yield
            tb = turn_bank.buf
            t = k.transposes([(tb[:, n * P:(n + 1) * P], src, k.ident[:, :])
                              for n, src in enumerate((qs.buf[:, :], kbs.buf[:, :], ks.buf[:, :]))],
                             [nq, nk, nb, turn_bank.free])
            qs.free = kbs.free = [t]
            qt, kq = qkT.next(), kq_bd.next()
            e1 = k.act(qt.buf[:, :, :].rearrange("p a t -> p (a t)"), tb[:, 0:2 * P], after=[t, qt.free, before])
            e2 = k.tt(kq.buf[:, :, :], tb[:, 2 * P:3 * P].rearrange("p (o t) -> p o t", o=1).to_broadcast([P, DH, P]),
                      bcast(k.mask_quad[:, :], P, DH), ALU.mult, [e1, kq.free, before])
            turn_bank.free = [e1, e2]
            yield
            pb = prod_bank.buf
            mm = []
            for n in (1, 0):
                for b_ in range(B):
                    rows_ = slice(CH * b_, CH * (b_ + 1))
                    mm.append((pb[rows_, (1 - n) * P:(2 - n) * P], qt.buf[:, n, rows_], kq.buf[:, :, rows_], True, True))
            m = k.matmuls(mm, [e1, e2, prod_bank.free])
            kq.free = [m]
            at, tt_ = attn.next(), attnT.next()
            a = k.tt(a_rows[:, ch % SOLVE, :, :], pb[:, 0:P].rearrange("p (h s) -> p h s", h=DH),
                     k.mask_a[:, :].rearrange("p (o s) -> p o s", o=1).to_broadcast([P, DH, CH]), ALU.mult,
                     [m, state["a_free"], before])
            f = k.tt(at.buf[:, :, :], pb[:, P:2 * P].rearrange("p (h s) -> p h s", h=DH),
                     k.mask_attn[:, :].rearrange("p (o s) -> p o s", o=1).to_broadcast([P, DH, CH]), ALU.mult,
                     [m, at.free, before])
            prod_bank.free = [a, f]
            tr = p.step("vector", lambda e_: e_.transpose(tt_.buf[:, :, :].rearrange("p h s -> p (h s)"),
                                                          at.buf[:, :, :].rearrange("p h s -> p (h s)")),
                        [f, tt_.free, before])
            at.free = [tr]
            kept[ch] = dict(k=(ks, nk), qk=(qt, e1), attn=(tt_, tr), bv=(bvs, v), gate=(gts, g2), a=a, h_read=mv,
                            qt_read=[m])
            yield

        def solve(n):
            chunks = range(n * SOLVE, (n + 1) * SOLVE)
            out = []
            for c in range(SOLVE):
                for b_ in range(B):
                    d = p.dma("sync", io["systems"][c, b_].rearrange("h t s -> t h s"), a_rows[b_ * CH:(b_ + 1) * CH, c, :, :],
                              a_out, [kept[chunks[c]]["a"], solved.get(n - 1, {}).get("loaded")])
            state["a_free"] = [d]
            sa, iv, pr = sys_a.next(), inv.next(), prod.next()
            ld = p.dma("sync", sa.buf[:, :, :], io["systems"].rearrange("c b h t s -> (c b h) t s"), a_in,
                       [d, sa.free, before])
            z = k.memset(iv.buf[:, :, :], 0.0, on="gpsimd", after=[iv.free, before])
            flat = iv.buf[:, :, :].rearrange("p s t -> p (s t)")
            last = k.memset(flat[:, 0:CH * CH:CH + 1], 1.0, on="gpsimd", after=[z])
            yield
            for i in range(1, CH):
                m = k.tt(pr.buf[:, 0:i, 0:i], iv.buf[:, 0:i, 0:i],
                         sa.buf[:, i, 0:i].rearrange("p (o j) -> p o j", o=1).to_broadcast([P, i, i]), ALU.mult,
                         [last, ld, pr.free, before])
                last = k.reduce(iv.buf[:, 0:i, i], pr.buf[:, 0:i, 0:i], ALU.add, after=[m])
                yield
            sa.free = [last]
            o = p.dma("sync", io["inverses"].rearrange("c b h s t -> (c b h) s t"), iv.buf[:, :, :], inv_out,
                      [last, solved.get(n - 1, {}).get("read")])
            iv.free = [o]
            solved[n] = dict(loaded=ld, out=o)

        def fetch(ch):
            s = invT.next()
            kpt = kept[ch]
            for b_ in range(B):
                rows_ = slice(CH * b_, CH * (b_ + 1))
                d = p.dma("sync", s.buf[rows_, :, rows_], io["inverses"][ch % SOLVE, b_].rearrange("h s t -> s h t"),
                          inv_in[invT.at], [solved[ch // SOLVE]["out"], s.free])
            kpt["inv"] = (s, d)
            solved[ch // SOLVE]["read"] = d
            ab = attn_bd.next()
            tt_, tr = kpt["attn"]
            done = k.tt(ab.buf[:, :, :].rearrange("p h (b t) -> p h b t", b=B),
                        tt_.buf[:, :, :].rearrange("p h (o t) -> p h o t", o=1).to_broadcast([P, DH, B, CH]),
                        k.mask_quad[:, :].rearrange("p (o b u) -> p o b u", o=1, u=1).to_broadcast([P, DH, B, CH]),
                        ALU.mult, [tr, ab.free, before], on="gpsimd")
            tt_.free = [done]
            kpt["attn_bd"] = (ab, done)

        s_written = [zeroed]
        updated = {}
        hold = {"u_free": [], "o": None}

        def scan(ch):
            kpt = kept[ch]
            (ks, nk), (qt, e1), (bvs, v), (gts, g2) = kpt["k"], kpt["qk"], kpt["bv"], kpt["gate"]
            (iv, iv_in), (ab, ab_in) = kpt["inv"], kpt["attn_bd"]
            cb, sb_, ob = chain_bank.buf, s_bank.buf, o_bank.buf
            rs, us = rhs.next(), u_rows.next()

            def by_batch(n, out, last):
                return [(out[CH * b_:CH * (b_ + 1), 0:HV], qt.buf[:, n, CH * b_:CH * (b_ + 1)],
                         s_bd[:, b_, :, :].rearrange("p h v -> p (h v)"), True, last) for b_ in range(B)]

            m = k.matmuls(by_batch(1, cb, True), [e1, s_written[0], chain_bank.free])
            mq = k.matmuls(by_batch(0, ob, False), [o_bank.free], lint=False)
            d = k.tt(rs.buf[:, :], bvs.buf[:, :], cb[:, 0:HV], ALU.subtract, [m, v, rs.free, before])
            bvs.free = [d]
            yield
            m = k.matmuls([(cb[:, HV + h * DV:HV + (h + 1) * DV], iv.buf[:, h, :], rs.buf[:, h * DV:(h + 1) * DV],
                            True, True) for h in range(DH)], [d, iv_in])
            rs.free = [m]
            iv.free = [m]
            ub, ur = [], []
            u4 = cb[:, HV:2 * HV].rearrange("p (h v) -> p h v", h=DH)
            for half, eng in enumerate(("scalar", "vector")):
                for b_ in (2 * half, 2 * half + 1):
                    rows_ = slice(CH * b_, CH * (b_ + 1))
                    ub.append(k.copy(u_bd[rows_, :, b_, :], u4[rows_, :, :], [m, hold["u_free"], zeroed], on=eng))
                rows_ = slice(64 * half, 64 * (half + 1))
                ur.append(k.copy(us.buf[rows_, :], cb[rows_, HV:2 * HV], [m, us.free, before], on=eng))
            chain_bank.free = ub + ur
            yield
            m = k.matmuls([(sb_[CH * h:CH * (h + 1), 0:HV], ks.buf[:, h * DK:(h + 1) * DK],
                            u_bd[:, h, :, :].rearrange("p b v -> p (b v)"), True, True) for h in range(DH)],
                          [ub, nk, s_bank.free])
            hold["u_free"] = [m]
            ks.free = [m]
            sw = []
            s4 = sb_[:, 0:HV].rearrange("p (b v) -> p b v", b=B)
            for h in range(DH):
                rows_ = slice(DK * h, DK * (h + 1))
                sw.append(k.tt(s_bd[rows_, :, h, :], s_bd[rows_, :, h, :], s4[rows_, :, :], ALU.add, [m, mq, s_written[0]]))
            s_written[0] = sw
            s_bank.free = sw
            mo = k.matmuls([(ob[:, h * DV:(h + 1) * DV], ab.buf[:, h, :], us.buf[:, h * DV:(h + 1) * DV], False, True)
                            for h in range(DH)], [ur, ab_in], lint=False)
            us.free = [mo]
            ab.free = [mo]
            qt.free = [mq] + kpt["qt_read"]
            yield
            o2, os_, ns = osq.next(), oss.next(), on.next()
            s = k.act(o2.buf[:, :], ob[:, 0:HV], ACT.Square, [mo, o2.free, before])
            r = k.reduce(os_.buf[:, :], o2.buf[:, :].rearrange("p (h v) -> p h v", h=DH), ALU.add,
                         after=[s, os_.free, before])
            o2.free = [r]
            a = k.ts(os_.buf[:, :], os_.buf[:, :], 1.0 / DV, EPS, ALU.mult, ALU.add, after=[r], on="gpsimd")
            q = k.tt(os_.buf[:, :], os_.buf[:, :], k.half_power[:, 0:DH], ALU.pow, [a], on="gpsimd")
            n = k.tt(ns.buf[:, :].rearrange("p (h v) -> p h v", h=DH), ob[:, 0:HV].rearrange("p (h v) -> p h v", h=DH),
                     bcast(os_.buf[:, :], DV, DH), ALU.mult, [q, ns.free, before])
            o_bank.free = [n]
            os_.free = [n]
            g = k.tt(ns.buf[:, :], ns.buf[:, :], gts.buf[:, :], ALU.mult, [n, g2], on="gpsimd")
            gts.free = [g]
            yield
            c = ch % TPG
            if c == 0:
                hold["o"] = oT.next()
                hold["o_done"] = []
            ot = hold["o"]
            t = k.transposes([(turn_bank.buf[:, kt * P:(kt + 1) * P], ns.buf[:, kt * P:(kt + 1) * P], k.ident[:, :])
                              for kt in range(KT)], [g, turn_bank.free])
            ns.free = [t]
            e = k.act(ot.buf[:, :, :, c, :], turn_bank.buf[:, 0:KT * P].rearrange("p (k b t) -> p k b t", k=KT, b=B),
                      after=[t, ot.free, before])
            turn_bank.free = [e]
            hold["o_done"].append(e)
            if c == TPG - 1:
                G = ch // TPG
                for b_ in range(B):
                    wb = prod_bank.buf[:, 0:C]
                    m = k.matmuls([(wb, ot.buf[:, kt, b_, :, :].rearrange("p c t -> p (c t)"), w_o[:, kt, :], kt == 0, kt == KT - 1)
                                   for kt in range(KT)], [hold["o_done"], prod_bank.free, w_in])
                    x = k.xr[:, b_ * QB + G, :]
                    a = k.tt(x, x, wb, ALU.add, [m])
                    prod_bank.free = [a]
                    updated[b_ * QB + G] = a
                    yield
                ot.free = [m]

        def run(gen):
            for _ in gen:
                pass

        def prepare(n):
            for G in range(n * SOLVE // TPG, (n + 1) * SOLVE // TPG):
                yield from prepare_group(G)

        run(prepare(0))
        run(solve(0))
        rounds = CHUNKS // SOLVE
        for n in range(rounds):
            def others(n=n):
                if n + 1 < rounds:
                    yield from prepare(n + 1)
                    yield from solve(n + 1)
            rest = others()
            for ch in range(n * SOLVE, (n + 1) * SOLVE):
                fetch(ch)
                for _ in scan(ch):
                    for _ in range(2):
                        next(rest, None)
            run(rest)
        k.ready = updated


def store_residual(k):
    p, io = k.p, k.io
    for g in range(GROUPS):
        a = p.arrival(f"out{g}")
        p.dma("sync", io["out"][g * BANK:(g + 1) * BANK, :].rearrange("(i p) c -> p i c", p=P),
              k.xr[:, g * TPG:(g + 1) * TPG, :], a, [k.ready[i] for i in range(g * TPG, (g + 1) * TPG)])


STAGES = {"attention": attention, "ffn": ffn, "delta": delta}


def build(nc, io, stages=("attention", "ffn", "delta", "ffn")):
    with ExitStack() as ctx:
        k = Kernel(nc, ctx, io)
        allocate(k)
        load_constants(k)
        if stages[0] != "attention":
            load_x(k)
        for n, s in enumerate(stages):
            STAGES[s](k)
        store_residual(k)
        k.p.run()




def constants():
    row, col = np.arange(P)[:, None], np.arange(P)[None, :]
    ch = np.arange(CH)[None, :]
    return np.concatenate([
        (row == col).astype(np.float32),
        np.where(col > row, np.float32(MASKED), np.float32(0)),
        np.where(ch < row % CH, np.float32(-1), np.float32(0)),
        (ch <= row % CH).astype(np.float32),
        (row // 32 == np.arange(4)[None, :]).astype(np.float32),
    ], axis=1)


def halves(w):
    return np.ascontiguousarray(w.reshape(KT, P, -1).transpose(1, 0, 2))


def lay_out(i):
    a = {n: np.asarray(v) for n, v in i.items()}
    A, D, F = "L0_attn_a_", "L0_attn_b_", "L0_ffn_"
    arrays = {
        "constants": constants(),
        "x": a[A + "x"].reshape(TOKENS, C),
        "wdqT": a[A + "W_dq"].T, "wuqT": a[A + "W_uq"].T, "wdkvT": a[A + "W_dkv"].T,
        "wuq": a[A + "W_uq"], "wuk": a[A + "W_uk"], "wdq": a[A + "W_dq"], "wuv": a[A + "W_uv"], "woT": a[A + "W_o"].T,
        "ffn_w": np.stack([halves(a[F + n].T) for n in ("wf", "wi", "wc", "wo", "uf", "ui", "uc", "uo")], axis=1),
        "ffn_b": np.stack([a[F + n].reshape(KT, P).T for n in ("bf", "bi", "bc", "in_c")], axis=1),
        "ffn_bo": a[F + "bo"].reshape(1, C),
        "d_qkb": halves(np.concatenate([a[D + "Wq"], a[D + "Wk"], a[D + "Wb"]], axis=1)),
        "d_vg": halves(np.concatenate([a[D + "Wv"], a[D + "Wg"]], axis=1)),
        "d_wo": halves(a[D + "Wo"]),
        "d_conv": halves(a[D + "conv_w"]),
        "d_norm": a[D + "norm_w"].reshape(1, DV),
    }
    return {n: np.ascontiguousarray(v) for n, v in arrays.items()}


def declare(nc, arrays):
    io = {n: nc.dram_tensor(f"in_{n}", v.shape, F32, kind="ExternalInput").ap() for n, v in arrays.items()}
    io["out"] = nc.dram_tensor("out_x", (TOKENS, C), F32, kind="ExternalOutput").ap()
    io["parts"] = nc.dram_tensor("qk_parts", (2, 3, C, TOKENS), BF16, kind="Internal").ap()
    io["systems"] = nc.dram_tensor("systems", (SOLVE, B, DH, CH, CH), F32, kind="Internal").ap()
    io["inverses"] = nc.dram_tensor("inverses", (SOLVE, B, DH, CH, CH), F32, kind="Internal").ap()
    return io


def kernel(**inputs):
    from concourse import bacc
    from concourse.bass_utils import run_bass_kernel_spmd

    arrays = lay_out(inputs)
    nc = bacc.Bacc("TRN2", target_bir_lowering=False, num_devices=1)
    io = declare(nc, arrays)
    build(nc, io)
    r = run_bass_kernel_spmd(nc, [{f"in_{n}": v for n, v in arrays.items()}], core_ids=[0])
    return r.results[0]["out_x"].reshape(B, T, C)
```

```python
from contextlib import ExitStack

import numpy as np

import concourse.bass as bass
from concourse import mybir

F32 = mybir.dt.float32
BF16 = mybir.dt.bfloat16
ALU = mybir.AluOpType
F32R = mybir.dt.float32r
ACT = mybir.ActivationFunctionType
AXIS_X = mybir.AxisListType.X

P = 128
B, T, C = 4, 1024, 256
TOKENS = B * T
TILES = TOKENS // P
KT = C // P
BANK = 512
GROUPS = TOKENS // BANK
TPG = BANK // P
EPS = 1e-5

NH, HS = 16, 16
HPU = 4
UNITS_PER_B = NH // HPU
QB = T // P
QC = T // BANK
SPLIT_Q = (0, 1, 0, 1, 2, 0)
SPLIT_K = (0, 0, 1, 1, 0, 2)
PRODUCTS = len(SPLIT_Q)
SCORE_ROWS = PRODUCTS * HS
MAX_ROWS = 3
STACKS = 3
MAX_LEAD = 16
MASKED = -float(2.0 ** 100)

DH, DK, DV = 4, 32, 64
CH = 32
CHUNKS = T // CH
SOLVE = P // (B * DH)
WINDOW = 2 * SOLVE

ENGINES = ("sync", "gpsimd", "tensor", "scalar", "vector")


class Step:

    def __init__(self, engine, emit, after, arrival=None):
        self.engine, self.emit, self.after, self.arrival = engine, emit, after, arrival
        self.signals, self.count = False, 0


class Program:

    def __init__(self, nc, ctx):
        self.nc, self.ctx = nc, ctx
        self.queue = {e: [] for e in ENGINES}
        self.done = {e: ctx.enter_context(nc.semaphore(f"{e}_done")) for e in ENGINES}
        self.arrivals = []

    def step(self, engine, emit, after=()):
        s = Step(engine, emit, [])
        self._wait_for(s, after)
        self.queue[engine].append(s)
        return s

    def _wait_for(self, s, after):
        for a in after:
            if a is None:
                continue
            if isinstance(a, (list, tuple)):
                self._wait_for(s, a)
                continue
            if a.arrival is None:
                a.signals = True
            s.after.append(a)

    def arrival(self, name):
        a = [self.ctx.enter_context(self.nc.semaphore(name)), 0]
        self.arrivals.append(a)
        return a

    def dma(self, engine, out, in_, arrival, after=()):
        arrival[1] += 16
        s = Step(engine, lambda e: e.dma_start(out, in_), [], (arrival[0], arrival[1]))
        self._wait_for(s, after)
        self.queue[engine].append(s)
        return s

    def tail(self):
        return [q[-1] for q in self.queue.values() if q]

    def run(self):
        for e in ENGINES:
            n = 0
            for s in self.queue[e]:
                if s.arrival is None and s.signals:
                    n += 1
                    s.count = n
        block = self.ctx.enter_context(self.nc.Block())
        enter = {"sync": block.sync, "gpsimd": block.gpsimd, "tensor": block.tensor, "scalar": block.scalar,
                 "vector": block.vector}
        for e in ENGINES:
            def body(eng, e=e):
                seen = {}
                for s in self.queue[e]:
                    for a in s.after:
                        sem, value, key = (self.done[a.engine], a.count, a.engine) if a.arrival is None else \
                            (a.arrival[0], a.arrival[1], id(a.arrival[0]))
                        if seen.get(key, 0) < value:
                            eng.wait_ge(sem, value)
                            seen[key] = value
                    ins = s.emit(eng)
                    if s.arrival is not None:
                        ins.then_inc(s.arrival[0], 16)
                    elif s.signals:
                        ins.then_inc(self.done[e], 1)
                if e == "sync":
                    for sem, total in self.arrivals:
                        if total:
                            eng.wait_ge(sem, total)
            enter[e](body)


class Slot:

    def __init__(self, buf):
        self.buf, self.free = buf, []


class Ring:
    def __init__(self, bufs):
        self.slots, self.at = [Slot(b) for b in bufs], -1

    def next(self):
        self.at = (self.at + 1) % len(self.slots)
        return self.slots[self.at]


class Kernel:
    def __init__(self, nc, ctx, io):
        self.nc, self.ctx, self.io = nc, ctx, io
        self.p = Program(nc, ctx)
        self.psum_pairs = [ctx.enter_context(nc.psum_tensor(f"psum{i}", [P, 2, BANK], F32)) for i in range(4)]
        self.bank = [Slot(pair[:, j, :]) for pair in self.psum_pairs for j in range(2)]

    def pe(self, emit, after=()):
        return self.p.step("tensor", emit, after)

    def act(self, out, in_, func=ACT.Copy, after=(), **kw):
        return self.p.step("scalar", lambda e: e.activation(out, in_, func, **kw), after)

    def tt(self, out, a, b, op, after=(), on="vector"):
        return self.p.step(on, lambda e: e.tensor_tensor(out, a, b, op), after)

    def ts(self, out, a, s1, s2, op0, op1=ALU.bypass, after=(), on="vector"):
        return self.p.step(on, lambda e: e.tensor_scalar(out, a, s1, s2, op0, op1), after)

    def copy(self, out, in_, after=(), on="vector"):
        if on == "scalar":
            return self.act(out, in_, after=after)
        return self.p.step(on, lambda e: e.tensor_copy(out, in_), after)

    def reduce(self, out, in_, op, negate=False, after=()):
        return self.p.step("vector", lambda e: e.tensor_reduce(out, in_, AXIS_X, op, negate=negate), after)

    def memset(self, out, value, on="gpsimd", after=()):
        return self.p.step(on, lambda e: e.memset(out, value), after)

    def matmuls(self, parts, after=(), lint=True):
        def emit(e):
            for out, lhsT, rhs, start, stop in parts:
                last = e.matmul(out, lhsT, rhs, start=start, stop=stop, skip_group_check=not lint)
            return last
        return self.pe(emit, after)

    def transposes(self, parts, after=()):
        def emit(e):
            for out, in_, ident in parts:
                last = e.transpose(out, in_, ident)
            return last
        return self.pe(emit, after)


def allocate(k):
    nc, ctx = k.nc, k.ctx

    def sb(name, shape, dt=F32):
        return ctx.enter_context(nc.sbuf_tensor(name, shape, dt))

    k.xr = sb("residual", [P, TILES, C])
    k.ident = sb("identity", [P, P])
    k.mask_scores = sb("mask_scores", [P, P])
    k.mask_a = sb("mask_strict", [P, CH])
    k.mask_attn = sb("mask_incl", [P, CH])
    k.mask_quad = sb("mask_quadrant", [P, 4])
    k.ident16 = sb("identity16", [P, P], BF16)
    k.mask16 = sb("mask_scores16", [P, P], BF16)
    k.half_power = sb("minus_half", [P, 2 * DH * TPG])
    k.ffn_w = sb("ffn_weights", [P, 8, KT, C])
    k.ffn_b = sb("ffn_biases", [P, 4, KT])
    k.ffn_bo = sb("ffn_bo", [P, C])
    k.stats = sb("ln_stats", [P, TILES, 6])
    k.moments = sb("ln_moments", [P, TILES, 2])
    k.rstd = sb("ln_rstd", [P, TILES])
    k.xn = Ring([sb(f"normed{i}", [P, TPG, C]) for i in range(3)])


def load_ffn_weights(k):
    p, io = k.p, k.io
    a_w, a_b = p.arrival("ffn_w_in"), p.arrival("ffn_b_in")
    w_in = p.dma("scalar", k.ffn_w[:, :, :, :], io["ffn_w"], a_w)
    p.dma("scalar", k.ffn_b[:, :, :], io["ffn_b"], a_b)
    b_in = p.dma("scalar", k.ffn_bo[:, :], io["ffn_bo"].to_broadcast([P, C]), a_b)
    k.ffn_in = (w_in, b_in)


def load_constants(k):
    p, io = k.p, k.io
    arrival = p.arrival("constants_in")
    at = 0
    for buf in (k.ident, k.mask_scores, k.mask_a, k.mask_attn, k.mask_quad):
        n = buf.shape[1]
        last = p.dma("scalar", buf[:, :], io["constants"][:, at:at + n], arrival)
        at += n
    k.constants = last
    a = k.copy(k.ident16[:, :], k.ident[:, :], [last])
    b = k.copy(k.mask16[:, :], k.mask_scores[:, :], [last])
    k.const16 = [a, b]
    k.powers = k.memset(k.half_power[:, :], -0.5)


def layernorm(k, tiles, ready):
    slot = k.xn.next()
    g = slice(tiles[0], tiles[-1] + 1, tiles[1] - tiles[0])
    out = []
    for i in tiles:
        s = k.p.step("vector", lambda e, i=i: e.bn_stats(k.stats[:, i, :], k.xr[:, i, :]), [ready[i]])
        m = k.p.step("vector", lambda e, i=i: e.bn_aggr(k.moments[:, i, :], k.stats[:, i, :]), [s])
    a = k.ts(k.rstd[:, g], k.moments[:, g, 1], EPS, None, ALU.add, after=[m], on="gpsimd")
    r = k.tt(k.rstd[:, g], k.rstd[:, g], k.half_power[:, 0:len(tiles)], ALU.pow, after=[a, k.powers], on="gpsimd")
    for j, i in enumerate(tiles):
        out.append(k.ts(slot.buf[:, j, :], k.xr[:, i, :], k.moments[:, i, 0:1], k.rstd[:, i:i + 1],
                        ALU.subtract, ALU.mult, after=[r, slot.free]))
    return slot, out


def turned(k, normed, banks, write):
    slot, steps = normed
    evacuated = []
    for kt in range(KT):
        bank = banks[kt % len(banks)]
        t = k.transposes([(bank.buf[:, j * P:(j + 1) * P], slot.buf[:, j, kt * P:(kt + 1) * P], k.ident[:, :])
                          for j in range(TPG)], [steps, bank.free, k.constants])
        done = write(kt, bank.buf, [t])
        bank.free = [done]
        evacuated.append(done)
    slot.free = [t]
    return evacuated


def attention(k):
    with ExitStack() as ctx:
        v_rows = ctx.enter_context(k.nc.sbuf_tensor("v_rows", [P, TILES, NH, HS + 1], F32))
        with ExitStack() as inner:
            parts_written, v_done = attention_project(k, inner, v_rows)
        attention_scores(k, ctx, v_rows, parts_written, v_done)


def load_x(k):
    k.ready = {}
    for g in range(GROUPS):
        a = k.p.arrival(f"x_in{g}")
        s = k.p.dma("sync", k.xr[:, g * TPG:(g + 1) * TPG, :],
                    k.io["x"][g * BANK:(g + 1) * BANK, :].rearrange("(i p) c -> p i c", p=P), a)
        for i in range(TPG):
            k.ready[g * TPG + i] = s


def attention_project(k, ctx, v_rows):
    nc, p, io = k.nc, k.p, k.io

    def sb(name, shape, dt=F32):
        return ctx.enter_context(nc.sbuf_tensor(name, shape, dt))

    w = {}
    arrived = {}
    for name, shape in (("wdqT", [P, KT, P]), ("wdkvT", [P, KT, P]), ("wuqT", [P, C]), ("wuq", [P, KT, P]),
                        ("wuk", [P, KT, P]), ("wdq", [P, C]), ("wuv", [P, KT, P]), ("woT", [P, KT, C])):
        w[name] = sb("a_" + name, shape)
        arrival = p.arrival(f"in_{name}")
        dst = w[name][:, :, :] if len(shape) == 3 else w[name][:, :]
        src = io[name]
        arrived[name] = p.dma("scalar", dst, src.rearrange("(a p) n -> p a n", p=P) if len(shape) == 3 else src, arrival)
    xT = Ring([sb(f"a_xT{i}", [P, KT, BANK]) for i in range(2)])
    lat = Ring([sb(f"a_latent{i}", [P, 2, BANK]) for i in range(2)])
    rest = Ring([sb(f"a_rest{i}", [P, BANK]) for i in range(4)])
    parts = Ring([sb(f"a_parts{i}", [P, 3, BANK], BF16) for i in range(4)])
    sent = [p.arrival(f"parts_out{i}") for i in range(4)]
    keff = sb("a_keffT", [P, C])
    veff = sb("a_veff", [P, C])
    wuk_q = sb("a_wuk_q", [P, P])

    load_ffn_weights(k)
    ring = Ring([])
    ring.slots = k.bank[2:8]
    b0 = ring.next()
    t1 = k.matmuls([(b0.buf[:, 0:P], w["wuq"][:, kt, :], w["wuk"][:, kt, :], kt == 0, kt == KT - 1) for kt in range(KT)],
                   [arrived["wuq"], arrived["wuk"]])
    t1c = k.copy(wuk_q[:, :], b0.buf[:, 0:P], [t1])
    b0.free = [t1c]
    b1 = ring.next()
    ke = k.matmuls([(b1.buf[:, 0:C], wuk_q[:, :], w["wdq"][:, :], True, True)], [t1c, arrived["wdq"]])
    kec = k.copy(keff[:, :], b1.buf[:, 0:C], [ke])
    b1.free = [kec]
    b2 = ring.next()
    ve = k.matmuls([(b2.buf[:, 0:C], w["wuv"][:, kt, :], w["woT"][:, kt, :], kt == 0, kt == KT - 1) for kt in range(KT)],
                   [arrived["wuv"], arrived["woT"]])
    vec = k.copy(veff[:, :], b2.buf[:, 0:C], [ve])
    b2.free = [vec]
    ones = k.memset(v_rows[:, :, :, HS:HS + 1], 1.0)

    load_x(k)
    x_in = k.ready
    written = {}
    v_done = []

    def tiles(g):
        return list(range(g * TPG, (g + 1) * TPG))

    def turn(normed):
        xs = xT.next()
        return xs, turned(k, normed, k.bank[0:2],
                          lambda kt, bank, after: k.copy(xs.buf[:, kt, :], bank[:, :], after + xs.free, on="vector"))

    normed = [layernorm(k, tiles(0), x_in), layernorm(k, tiles(1), x_in)]
    ahead = turn(normed.pop(0))
    for g in range(GROUPS):
        cols = slice(g * BANK, (g + 1) * BANK)
        xs, evac = ahead
        if g + 2 < GROUPS:
            normed.append(layernorm(k, tiles(g + 2), x_in))
        ls = lat.next()
        lat_done = []
        for n, name in enumerate(("wdqT", "wdkvT")):
            bk = ring.next()
            m = k.matmuls([(bk.buf[:, :], w[name][:, kt, :], xs.buf[:, kt, :], kt == 0, kt == KT - 1) for kt in range(KT)],
                          [evac, bk.free, arrived[name]])
            e = k.copy(ls.buf[:, n, :], bk.buf[:, :], [m, ls.free], on="scalar")
            bk.free = [e]
            lat_done.append(e)
        xs.free = [m]
        if g + 1 < GROUPS:
            ahead = turn(normed.pop(0))
        readers = []
        for which, (weight, ready) in enumerate((("q", arrived["wuqT"]), ("k", kec))):
            for mt in range(KT):
                lhsT = w["wuqT"][:, mt * P:(mt + 1) * P] if weight == "q" else keff[:, mt * P:(mt + 1) * P]
                bk = ring.next()
                m = k.matmuls([(bk.buf[:, :], lhsT, ls.buf[:, which, :], True, True)], [lat_done[which], bk.free, ready])
                readers.append(m)
                ps, rs = parts.next(), rest.next()
                hi = k.copy(ps.buf[:, 0, :], bk.buf[:, :], [m, ps.free], on="scalar")
                r = k.tt(rs.buf[:, :], bk.buf[:, :], ps.buf[:, 0, :], ALU.subtract, [hi, rs.free])
                bk.free = [r]
                mid = k.copy(ps.buf[:, 1, :], rs.buf[:, :], [r], on="scalar")
                lo = k.tt(ps.buf[:, 2, :], rs.buf[:, :], ps.buf[:, 1, :], ALU.subtract, [mid], on="gpsimd")
                rs.free = [lo]
                d = p.dma("sync", io["parts"][which, :, mt * P:(mt + 1) * P, cols].rearrange("s c t -> c s t"),
                          ps.buf[:, :, :], sent[parts.at], [lo])
                ps.free = [d]
                written.setdefault(g // QC, []).append(d)
        for j in range(0, TPG, 2):
            bk = ring.next()
            m = k.matmuls([(bk.buf[:, n * C:(n + 1) * C], ls.buf[:, 1, (j + n) * P:(j + n + 1) * P], veff[:, :], True, True)
                           for n in range(2)], [lat_done[1], vec, bk.free])
            i = g * TPG + j
            e = k.copy(v_rows[:, i:i + 2, :, 0:HS], bk.buf[:, :].rearrange("p (i h d) -> p i h d", i=2, h=NH), [m],
                       on="scalar")
            bk.free = [e]
            v_done.append(e)
        ls.free = readers + [m]
    return written, v_done + [ones]


def attention_scores(k, ctx, v_rows, parts_written, v_done):
    nc, p, io = k.nc, k.p, k.io
    before = p.tail()

    def sb(name, shape, dt=F32):
        return ctx.enter_context(nc.sbuf_tensor(name, shape, dt))

    qst = [sb(f"q_stack{i}", [P, HPU, T], BF16) for i in range(STACKS)]
    kst = [sb(f"k_stack{i}", [P, HPU, T], BF16) for i in range(STACKS)]
    weights = [sb(f"weights{i}", [P, HPU, BANK]) for i in range(2)]
    maxima = [sb(f"maxima{i}", [P, HPU, QB, 2]) for i in range(2)]
    negmax = [sb(f"negmax{i}", [P, HPU * QB]) for i in range(2)]
    mparts = [sb(f"max_parts{i}", [HPU * QB, MAX_ROWS, P], BF16) for i in range(2)]
    mrest = [sb(f"max_rest{i}", [HPU * QB, P]) for i in range(2)]
    oT = Ring([sb(f"att_oT{i}", [P, BANK]) for i in range(2)])
    rden = Ring([sb(f"att_rden{i}", [P, TPG, HPU]) for i in range(2)])
    onorm = Ring([sb(f"att_o{i}", [P, TPG, HPU, HS]) for i in range(2)])
    st_banks = [k.bank[0:2], k.bank[2:4]]
    max_ring = Ring([])
    max_ring.slots = k.bank[4:7]
    o_bank = k.bank[7]

    st_free = [[b.free for b in k.bank[0:2]], [b.free for b in k.bank[2:4]]]
    zero = k.memset(o_bank.buf[:, :], 0.0, on="vector", after=[o_bank.free, before])
    o_bank.free = [zero]
    arrived_stack = [p.arrival(f"stack_in{i}") for i in range(STACKS)]
    arrived_max = [p.arrival(f"max_in{i}") for i in range(STACKS)]
    ones = [k.memset(kst[s][SCORE_ROWS:SCORE_ROWS + MAX_ROWS, :, :], 1.0, on="vector", after=[before])
            for s in range(STACKS)]

    units = [(b, g) for b in range(B) for g in range(UNITS_PER_B)]
    stack_done, max_done, stack_free = {}, {}, {}
    readers = {}

    def load(u):
        b, g = units[u]
        s = u % STACKS
        for n in range(PRODUCTS):
            for which, dst, part in ((0, qst[s], SPLIT_Q[n]), (1, kst[s], SPLIT_K[n])):
                src = io["parts"][which, part, g * HPU * HS:(g + 1) * HPU * HS, b * T:(b + 1) * T]
                d = p.dma("sync", dst[n * HS:(n + 1) * HS, :, :], src.rearrange("(h d) t -> d h t", h=HPU),
                          arrived_stack[s], [before, parts_written[b], stack_free.get(u - STACKS)])
        stack_done[u] = d

    per_unit = [(h, qb, c * BANK, min(BANK, (qb + 1) * P - c * BANK)) for qb in range(QB) for h in range(HPU)
                for c in range((qb + 1) * P // BANK + ((qb + 1) * P % BANK > 0))]
    max_tiles = [(u, *t) for u in range(len(units)) for t in per_unit]
    state = {"at": 0}
    reduced = {}

    def max_tile():
        if state["at"] == len(max_tiles):
            return
        u, h, qb, k0, w = max_tiles[state["at"]]
        first = state["at"] % len(per_unit) == 0
        state["at"] += 1
        s = u % STACKS
        if first:
            reduced[u] = []
        bk = max_ring.next()
        lhsT = qst[s][0:SCORE_ROWS, h, qb * P:(qb + 1) * P]
        diagonal = k0 + w == (qb + 1) * P
        mm = [(bk.buf[:, 0:w], lhsT, kst[s][0:SCORE_ROWS, h, k0:k0 + w], True, not diagonal)]
        if diagonal:
            mm.append((bk.buf[:, w - P:w], k.ident16[:, :], k.mask16[:, :], False, True))
        m = k.matmuls(mm, [stack_done[u], bk.free, k.const16])
        r = k.reduce(maxima[u % 2][:, h, qb, k0 // BANK:k0 // BANK + 1], bk.buf[:, 0:w], ALU.max, negate=True,
                     after=[m, readers.get(("max", u - 2))])
        bk.free = [r]
        reduced[u].append(r)
        if len(reduced[u]) == len(per_unit):
            finish_max(u)

    def finish_max(u):
        n, s = u % 2, u % STACKS
        half = QB // 2
        nm = negmax[n][:, :].rearrange("p (h q) -> p h q", h=HPU)
        free = readers.get(("max", u - 2), [])
        a = k.copy(nm[:, :, 0:half], maxima[n][:, :, 0:half, 0], [reduced[u], free])
        c = k.tt(nm[:, :, half:QB], maxima[n][:, :, half:QB, 0], maxima[n][:, :, half:QB, 1], ALU.min, [reduced[u], free])
        misc = max_ring.next()
        rows = misc.buf[0:HPU * QB, 0:P]
        t = k.transposes([(rows, negmax[n][:, :], k.ident[:, :])], [a, c, misc.free])
        hi = k.copy(mparts[n][:, 0, :], rows, [t, readers.get(("mparts", u - 2))])
        r = k.tt(mrest[n][:, :], rows, mparts[n][:, 0, :], ALU.subtract, [hi])
        misc.free = [r]
        mid = k.copy(mparts[n][:, 1, :], mrest[n][:, :], [r])
        lo = k.tt(mparts[n][:, 2, :], mrest[n][:, :], mparts[n][:, 1, :], ALU.subtract, [mid])
        for j in range(MAX_ROWS):
            dst = qst[s][SCORE_ROWS + j:SCORE_ROWS + j + 1, :, :].rearrange("o h (q t) -> o (h q) t", q=QB)
            d = p.dma("sync", dst, mparts[n][:, j, :], arrived_max[s], [lo, stack_free.get(u - STACKS)])
        max_done[u] = d
        readers[("max", u)] = [t, a, c]
        readers[("mparts", u)] = [d]

    exp_done = {}
    w_free = [[], []]
    o_state = {"free": o_bank.free}

    def score_pair(u, step, kb, qc, pair):
        s = u % STACKS
        q0 = max(qc * BANK, kb * P)
        w = (qc + 1) * BANK - q0
        mm = []
        for j in range(2):
            h = 2 * pair + j
            diagonal = kb * P >= qc * BANK
            out = st_banks[pair][j].buf
            mm.append((out[:, 0:w], kst[s][0:SCORE_ROWS + MAX_ROWS, h, kb * P:(kb + 1) * P],
                       qst[s][0:SCORE_ROWS + MAX_ROWS, h, q0:q0 + w], True, not diagonal))
            if diagonal:
                mm.append((out[:, 0:P], k.mask16[:, :], k.ident16[:, :], False, True))
        m = k.matmuls(mm, [stack_done[u], max_done[u], ones[s], st_free[pair], k.const16])
        last_scores[u] = m
        slot = step % 2
        src = st_pair[pair][:, :, 0:w]
        e = k.act(weights[slot][:, 2 * pair:2 * pair + 2, 0:w], src, ACT.Exp, [m, w_free[slot], before], scale=HS ** -0.5)
        st_free[pair] = [e]
        return e, w, q0 - qc * BANK

    last_scores = {}
    first_out = [True]

    def values(u, step, kb, qc, exps, w, off):
        b, _ = units[u]
        g = units[u][1]
        slot = step % 2
        last_kb = kb == (qc + 1) * TPG - 1
        mm = [(o_bank.buf[32 * h:32 * h + HS + 1, off:off + w], v_rows[:, b * QB + kb, g * HPU + h, :],
               weights[slot][:, h, 0:w], kb == 0, last_kb) for h in range(HPU)]
        m = k.matmuls(mm, [exps, v_done, o_state["free"] if kb == 0 else None])
        w_free[slot] = [m]
        if last_kb:
            os_ = oT.next()
            e = k.copy(os_.buf[:, :], o_bank.buf[:, :], [m, os_.free], on="scalar")
            o_state["free"] = [e]
            return (u, qc, os_, e)

    updated = {}

    def output(u, qc, os_, e):
        b, g = units[u]
        misc = max_ring.next()
        t = k.transposes([(misc.buf[:, j * P:(j + 1) * P], os_.buf[:, j * P:(j + 1) * P], k.ident[:, :])
                          for j in range(TPG)], [e, misc.free])
        os_.free = [t]
        rows = misc.buf[:, :].rearrange("p (i h d) -> p i h d", i=TPG, h=HPU)
        rs, ns = rden.next(), onorm.next()
        r = k.p.step("vector", lambda en: en.reciprocal(rs.buf[:, :, :], rows[:, :, :, HS]), [t, rs.free])
        mul = k.tt(ns.buf[:, :, :, :], rows[:, :, :, 0:HS],
                   rs.buf[:, :, :].rearrange("p i (h o) -> p i h o", o=1).to_broadcast([P, TPG, HPU, HS]),
                   ALU.mult, [r, ns.free])
        misc.free = [mul]
        rs.free = [mul]
        i = b * QB + qc * TPG
        x = k.xr[:, i:i + TPG, g * HPU * HS:(g + 1) * HPU * HS]
        a = k.tt(x, x, ns.buf[:, :, :, :].rearrange("p i h d -> p i (h d)"), ALU.add, [mul, before], on="gpsimd")
        ns.free = [a]
        for j in range(TPG):
            updated[i + j] = a

    st_pair = [k.psum_pairs[0], k.psum_pairs[1]]
    for u in range(min(STACKS, len(units))):
        load(u)
    lead = len(per_unit) + MAX_LEAD
    for _ in range(lead):
        max_tile()
    steps = [(u, kb, qc) for u in range(len(units)) for qc in range(QC) for kb in range((qc + 1) * TPG)]
    per_step = len(per_unit) // (len(steps) // len(units))
    pending, finishing = None, None
    for n, (u, kb, qc) in enumerate(steps):
        new_unit = n % (len(steps) // len(units)) == 0
        e0, w, off = score_pair(u, n, kb, qc, 0)
        max_tile()
        e1, w, off = score_pair(u, n, kb, qc, 1)
        max_tile()
        if finishing:
            output(*finishing)
            finishing = None
        max_tile()
        if pending:
            finishing = values(*pending)
            if new_unit:
                done = u - 1
                stack_free[done] = [last_scores[done]]
                if done + STACKS < len(units):
                    load(done + STACKS)
        pending = (u, n, kb, qc, [e0, e1], w, off)
        for _ in range(per_step - 3):
            max_tile()
    if finishing:
        output(*finishing)
    output(*values(*pending))
    o_bank.free = o_state["free"]
    for n in range(2):
        for j in range(2):
            k.bank[2 * n + j].free = st_free[n]
    k.ready = updated


def split(k, hi, lo, src, after, hi_on="scalar", lo_on="vector"):
    h = k.copy(hi, src, after, on=hi_on)
    l = k.tt(lo, src, hi, ALU.subtract, [h], on=lo_on)
    return [h, l]


PRODUCTS_R = ((0, 0), (0, 1), (1, 0))


def ffn(k):
    nc, p, io = k.nc, k.p, k.io
    before = p.tail()
    tag = f"f{len(p.arrivals)}_"
    with ExitStack() as ctx:
        def sb(name, shape, dt=F32):
            return ctx.enter_context(nc.sbuf_tensor(tag + name, shape, dt))

        bias, bo = k.ffn_b, k.ffn_bo
        w_in, b_in = k.ffn_in
        w_hi = sb("weights_hi", [P, 8, KT, C], F32R)
        w_lo = sb("weights_lo", [P, 8, KT, C], F32R)
        w_parts = (w_hi, w_lo)
        bias0 = sb("first_biases", [P, 3, KT])
        init = bias[:, 3, :]
        xT = Ring([sb(f"xT{i}", [P, 2, KT, BANK], F32R) for i in range(3)])
        gates = Ring([sb(f"gates{i}", [P, 3, KT, BANK]) for i in range(2)])
        state = [sb(f"state{j}", [P, KT, BANK]) for j in range(QC)]
        state_parts = [sb(f"state_parts{j}", [P, 2, KT, BANK], F32R) for j in range(QC)]
        cu_slot = gates.slots[0]
        cu = [cu_slot.buf[:, j, :, :].rearrange("p k (i c) -> p (k i) c", c=C) for j in range(QC)]
        hidden = sb("hidden", [P, TILES, C])

        ln_banks = k.bank[0:2]
        ring = Ring([])
        ring.slots = k.bank[2:8]

        normed, rows = {}, {}

        def norm_rows(g):
            if g < GROUPS:
                rows[g] = layernorm(k, list(range(g * TPG, (g + 1) * TPG)), k.ready)

        def norm_turn(g):
            if g < GROUPS:
                x = xT.next()
                steps = turned(k, rows[g], ln_banks, lambda kt, bank, after: split(
                    k, x.buf[:, 0, kt, :], x.buf[:, 1, kt, :], bank[:, :], [after, before, x.free]))
                normed[g] = (x, steps)

        for g in range(2):
            norm_rows(g)

        bk = ring.next()
        m = k.matmuls([(bk.buf[:, 2 * g + mt:2 * g + mt + 1], k.ffn_w[:, 4 + g, kt, mt * P:(mt + 1) * P],
                        init[:, kt:kt + 1], kt == 0, kt == KT - 1)
                       for g in range(3) for mt in range(KT) for kt in range(KT)], [w_in, b_in, bk.free])
        first_bias = k.tt(bias0[:, :, :], bk.buf[:, 0:6].rearrange("p (g m) -> p g m", g=3), bias[:, 0:3, :], ALU.add,
                          [m, before])
        bk.free = [first_bias]
        w_ready = {}

        def split_weights(n):
            w_ready[n] = split(k, w_hi[:, n, :, :], w_lo[:, n, :, :], k.ffn_w[:, n, :, :], [w_in, before, m])

        for n in range(3):
            split_weights(n)
        for g in range(2):
            norm_turn(g)
        for n in range(3, 8):
            split_weights(n)
        norm_rows(2)

        written = [None] * QC

        def recur(t, j, between=lambda gate: None):
            x, x_ready = normed[t * QC + j]
            gs = gates.next()
            parts = []
            for gate, func in ((0, ACT.Sigmoid), (1, ACT.Sigmoid), (2, ACT.Tanh)):
                for mt in range(KT):
                    bk = ring.next()
                    ms = slice(mt * P, (mt + 1) * P)
                    terms = [(w, v, kt) for kt in range(KT) for w, v in PRODUCTS_R]
                    m = k.matmuls([(bk.buf[:, :], w_parts[w][:, gate, kt, ms], x.buf[:, v, kt, :],
                                    i == 0, t == 0 and i == len(terms) - 1) for i, (w, v, kt) in enumerate(terms)],
                                  [x_ready, w_ready[gate], bk.free])
                    if t:
                        m = k.matmuls([(bk.buf[:, :], w_parts[w][:, 4 + gate, kt, ms], state_parts[j][:, v, kt, :],
                                        False, i == len(terms) - 1) for i, (w, v, kt) in enumerate(terms)],
                                      [written[j], w_ready[4 + gate]])
                    b = (bias if t else bias0)[:, gate, mt:mt + 1]
                    a = k.act(gs.buf[:, gate, mt, :], bk.buf[:, :], func, [m, first_bias, gs.free, before], bias=b)
                    bk.free = [a]
                    parts.append(a)
                between(gate)
            for half in range(2):
                bk = ring.next()
                i = (t * QC + j) * TPG + 2 * half
                terms = [(w, v, kt) for kt in range(KT) for w, v in PRODUCTS_R]
                mo = k.matmuls([(bk.buf[:, n * C:(n + 1) * C], x.buf[:, v, kt, (2 * half + n) * P:(2 * half + n + 1) * P],
                                 w_parts[w][:, 3, kt, :], q == 0, q == len(terms) - 1)
                                for n in range(2) for q, (w, v, kt) in enumerate(terms)],
                               [x_ready, w_ready[3], bk.free])
                bk.free = [k.copy(hidden[:, i:i + 2, :], bk.buf[:, :].rearrange("p (n c) -> p n c", n=2),
                                  [mo, before], on="scalar" if half else "vector")]
                hidden_written[i] = hidden_written[i + 1] = bk.free[0]
            x.free = [mo]
            norm_rows(t * QC + j + 3)
            kept = []
            if t:
                kept.append(k.tt(gs.buf[:, 0, :, :], gs.buf[:, 0, :, :], state[j][:, :, :], ALU.mult, [parts, written[j]]))
            else:
                for mt in range(KT):
                    kept.append(k.ts(gs.buf[:, 0, mt, :], gs.buf[:, 0, mt, :], init[:, mt:mt + 1], None, ALU.mult,
                                     after=[parts, b_in]))
            fresh = k.tt(gs.buf[:, 1, :, :], gs.buf[:, 1, :, :], gs.buf[:, 2, :, :], ALU.mult, [parts], on="gpsimd")
            w = k.tt(state[j][:, :, :], gs.buf[:, 0, :, :], gs.buf[:, 1, :, :], ALU.add, [kept, fresh, before])
            gs.free = [w]
            written[j] = [split(k, state_parts[j][:, 0, kt, :], state_parts[j][:, 1, kt, :], state[j][:, kt, :],
                                [w, m, before], hi_on="vector") for kt in range(KT)]

        updated, hidden_written = {}, {}

        def state_output(j):
            done = []
            for half in range(2):
                bk = ring.next()
                terms = [(w, v, kt) for kt in range(KT) for w, v in PRODUCTS_R]
                m = k.matmuls([(bk.buf[:, n * C:(n + 1) * C],
                                state_parts[j][:, v, kt, (2 * half + n) * P:(2 * half + n + 1) * P],
                                w_parts[w][:, 7, kt, :], q == 0, q == len(terms) - 1)
                               for n in range(2) for q, (w, v, kt) in enumerate(terms)], [written[j], w_ready[7], bk.free])
                a = k.tt(cu[j][:, 2 * half:2 * half + 2, :], bk.buf[:, :].rearrange("p (n c) -> p n c", n=2),
                         bo[:, :].rearrange("p (o c) -> p o c", o=1).to_broadcast([P, 2, C]), ALU.add, [m, b_in, cu_slot.free])
                bk.free = [a]
                done.append(a)
            return done

        def output(t, j, cu_done):
            i = (t * QC + j) * TPG
            h = hidden[:, i:i + TPG, :]
            s = k.tt(h, h, cu[j][:, :, :], ALU.add, [hidden_written[i], hidden_written[i + 2], cu_done])
            a = k.act(h, h, ACT.Tanh, [s])
            for n in range(TPG):
                x = k.xr[:, i + n, :]
                updated[i + n] = k.tt(x, x, hidden[:, i + n, :], ALU.add, [a], on="gpsimd" if n == 3 else "vector")

        def finish_first_half(gate):
            if gate == 0:
                out_done.append(state_output(0))
            else:
                output(gate - 1, 0, out_done[0])

        out_done = []
        for t in range(B):
            for j in range(QC):
                last = t == B - 1 and j == QC - 1
                recur(t, j, finish_first_half if last else lambda gate: None)
                norm_turn((t + 1) * QC + j)
        for t in range(2, B):
            output(t, 0, out_done[0])
        cu_done = state_output(1)
        for t in range(B):
            output(t, 1, cu_done)
        k.ready = updated


def delta(k):
    nc, p, io = k.nc, k.p, k.io
    before = p.tail()
    with ExitStack() as ctx:
        def sb(name, shape, dt=F32):
            return ctx.enter_context(nc.sbuf_tensor("d_" + name, shape, dt))

        def ring(name, n, shape):
            return Ring([sb(f"{name}{i}", shape) for i in range(n)])

        NQ = 2 * DH * DK
        QK = DH * DK
        HV = DH * DV
        w_qkb = sb("w_qkb", [P, KT, NQ + DH])
        w_vg = sb("w_vg", [P, KT, 2 * HV])
        w_o = sb("w_o", [P, KT, C])
        conv = sb("conv", [P, KT, 4])
        norm_w = sb("norm_w", [P, KT])
        a_w = p.arrival("delta_w_in")
        for dst, src in ((w_qkb[:, :, :], io["d_qkb"]), (w_vg[:, :, :], io["d_vg"]), (w_o[:, :, :], io["d_wo"]),
                         (conv[:, :, :], io["d_conv"]), (norm_w[:, :], io["d_norm"])):
            w_in = p.dma("sync", dst, src, a_w, [before])
        wo_scaled = [k.ts(w_o[:, kt, :], w_o[:, kt, :], norm_w[:, kt:kt + 1], None, ALU.mult, after=[w_in])
                     for kt in range(KT)]

        TAPS = 4
        xg = ring("xT", 2, [P, KT, B, TAPS - 1 + P])
        acc = ring("conv_sum", 1, [P, B * P])
        sig = ring("conv_sig", 1, [P, B * P])
        hT = ring("hT", 2, [P, KT, TPG, B, CH])
        qk = ring("qk_rows", 2 * TPG, [P, NQ])
        sq = ring("squares", 1, [P, NQ])
        ss = ring("sumsq", 2, [P, TPG, 2 * DH])
        qn = ring("q_normed", 2, [P, QK])
        kb = ring("k_beta", 2, [P, QK])
        beta = ring("beta", 2 * TPG, [P, DH])
        kq_bd = ring("kT_quads", 1, [P, DH, P])
        attn = ring("attn", 2, [P, DH, CH])
        a_rows = ring("a_rows", 2, [P, DH, CH])
        kn = ring("k_normed", WINDOW, [P, QK])
        qkT = ring("q_kb_T", WINDOW, [P, 2, P])
        attnT = ring("attnT", WINDOW, [P, DH, CH])
        bv = ring("beta_v", WINDOW, [P, HV])
        gate = ring("gate", WINDOW, [P, HV])
        sys_a = ring("systems", 1, [P, CH, CH])
        inv = ring("inverse", 1, [P, CH, CH])
        spare = k.xn.slots.pop()
        prod = Ring([spare.buf[:, :, :].rearrange("p a (b c) -> p (a b) c", c=CH)])
        prod.slots[0].free = spare.free
        invT = ring("inverses", 3, [P, DH, CH])
        inv_bd = ring("inv_quads", 2, [P, DH, P])
        s_bd = sb("state_quads", [P, B, DH, DV])
        rhs = ring("rhs", 1, [P, HV])
        u_bd = sb("u_quads", [P, DH, B, DV])
        osq = ring("o_squares", 1, [P, HV])
        oss = ring("o_sumsq", 2, [P, TPG, DH])
        on = ring("o_rows", 2, [P, TPG, HV])
        oT = ring("oT", 1, [P, KT, B, TPG, CH])

        zeroed = [k.memset(s_bd[:, :, :, :], 0.0, on="gpsimd", after=[before]),
                  k.memset(u_bd[:, :, :, :], 0.0, on="gpsimd", after=[before])]
        first_pad = k.memset(xg.slots[0].buf[:, :, :, 0:TAPS - 1], 0.0, on="gpsimd", after=[before])
        ln_bank, qk_bank, vg_bank, turn_bank, prod_bank, chain_bank, s_bank, o_bank = k.bank
        a_out = [p.arrival(f"systems_out{i}") for i in range(2)]
        a_in = p.arrival("systems_in")
        inv_out = p.arrival("inverses_out")
        inv_in = [p.arrival(f"inverse_in{i}") for i in range(4)]

        kept, fronts = {}, {}
        solved = {}
        state = {"pad": first_pad, "x_ready": None, "evacuated": 0, "prepared": 0}

        def bcast(ap, n, at):
            return ap.rearrange("p (x o) -> p x o", o=1).to_broadcast([P, at, n])

        def front(G):
            xs = xg.next()
            tiles = [b * QB + G for b in range(B)]
            prev = xg.slots[(xg.at - 1) % 2]
            if G:
                pad = k.copy(xs.buf[:, :, :, 0:TAPS - 1], prev.buf[:, :, :, P:P + TAPS - 1], [state["x_ready"], xs.free],
                             on="gpsimd")
            else:
                pad = state["pad"]
            evac = turned(
                k, layernorm(k, tiles, k.ready), [ln_bank],
                lambda kt, bank, after: k.act(xs.buf[:, kt, :, TAPS - 1:TAPS - 1 + P],
                                              bank[:, :].rearrange("p (b t) -> p b t", b=B),
                                              after=after + xs.free + before))
            state["x_ready"] = evac
            yield
            hs = hT.next()
            h_done = []
            for kt in range(KT):
                ac, sg = acc.next(), sig.next()
                a3 = ac.buf[:, :].rearrange("p (b t) -> p b t", b=B)
                s = k.ts(a3, xs.buf[:, kt, :, 0:P], conv[:, kt, 0:1], None, ALU.mult,
                         after=[evac, pad, w_in, ac.free, before])
                for i in range(1, TAPS):
                    s = p.step("vector", lambda e, i=i, a3=a3, kt=kt: e.scalar_tensor_tensor(
                        out=a3, in0=xs.buf[:, kt, :, i:i + P], scalar=conv[:, kt, i:i + 1], in1=a3,
                        op0=ALU.mult, op1=ALU.add), [s])
                    if i == 2:
                        yield
                g = k.act(sg.buf[:, :], ac.buf[:, :], ACT.Sigmoid, [s, sg.free, before])
                m = k.tt(hs.buf[:, kt, :, :, :].rearrange("p c b t -> p b c t"),
                         ac.buf[:, :].rearrange("p (b c t) -> p b c t", b=B, c=TPG),
                         sg.buf[:, :].rearrange("p (b c t) -> p b c t", b=B, c=TPG), ALU.mult, [g, hs.free, before],
                         on="gpsimd")
                ac.free = sg.free = [m]
                h_done.append(m)
                yield
            xs.free = [s] + ([pad] if G else [])
            state["pad_reader"] = s
            sss, got = ss.next(), []
            for c in range(TPG):
                got.append(project_qk(hs, c, h_done, sss))
                yield
            mx = k.ts(sss.buf[:, :, :], sss.buf[:, :, :], 1e-24, None, ALU.max, after=[x["sum"] for x in got], on="gpsimd")
            rn = k.tt(sss.buf[:, :, :], sss.buf[:, :, :],
                      k.half_power[:, 0:2 * DH * TPG].rearrange("p (c h) -> p c h", c=TPG), ALU.pow, [mx], on="gpsimd")
            fronts[G] = dict(hs=hs, h_done=h_done, got=got, sss=sss, rn=rn)

        def back(ch):
            G, c = ch // TPG, ch % TPG
            x = fronts[G]
            yield from prepare_chunk(ch, x["hs"], c, x["h_done"], x["got"][c], x["sss"], x["rn"])

        def prepare():
            active, ahead, ch = [], front(0), 0
            while ch < CHUNKS or active:
                if ch < CHUNKS and state["evacuated"] > ch - WINDOW:
                    if ch % TPG == 0:
                        for _ in ahead:
                            yield
                        ahead = front(ch // TPG + 1) if ch + TPG < CHUNKS else iter(())
                    active.append([back(ch), 0, ch])
                    ch += 1
                elif not active:
                    yield
                for a in list(active):
                    next(a[0])
                    a[1] += 1
                    if a[1] == 3:
                        active.remove(a)
                        state["prepared"] += 1
                        if a[2] % TPG == TPG - 1:
                            x = fronts[a[2] // TPG]
                            x["sss"].free = [kept[a[2]]["k"][1]]
                            x["hs"].free = [kept[a[2]]["h_read"]]
                    yield
                    next(ahead, None)

        def columns(hs, c):
            return [hs.buf[:, kt, c, :, :].rearrange("p b t -> p (b t)") for kt in range(KT)]

        def project_qk(hs, c, h_done, sss):
            cols, ps = columns(hs, c), qk_bank.buf
            m = k.matmuls([(ps[:, 0:NQ + DH], cols[kt], w_qkb[:, kt, :], kt == 0, kt == KT - 1) for kt in range(KT)],
                          [h_done, w_in, qk_bank.free])
            be, rows, sqs = beta.next(), qk.next(), sq.next()
            b = k.act(be.buf[:, :], ps[:, NQ:NQ + DH], ACT.Sigmoid, [m, be.free, before])
            e = k.act(rows.buf[:, :], ps[:, 0:NQ], after=[m, rows.free, before])
            q2 = k.act(sqs.buf[:, :], ps[:, 0:NQ], ACT.Square, after=[m, sqs.free, before])
            qk_bank.free = [q2]
            r = k.reduce(sss.buf[:, c, :], sqs.buf[:, :].rearrange("p (h d) -> p h d", d=DK), ALU.add,
                         after=[q2, sss.free, before])
            sqs.free = [r]
            return dict(beta=(be, b), rows=(rows, e), sum=r)

        def prepare_chunk(ch, hs, c, h_done, got, sss, rn):
            (be, b), (rows, e), cols = got["beta"], got["rows"], columns(hs, c)
            vg = vg_bank.buf
            mv = k.matmuls([(vg[:, :], cols[kt], w_vg[:, kt, :], kt == 0, kt == KT - 1) for kt in range(KT)],
                           [h_done, w_in, vg_bank.free])
            qs, ks, kbs = qn.next(), kn.next(), kb.next()

            def heads(ap):
                return ap.rearrange("p (h d) -> p h d", d=DK)

            nq = k.tt(heads(qs.buf[:, :]), heads(rows.buf[:, 0:QK]), bcast(sss.buf[:, c, 0:DH], DK, DH), ALU.mult,
                      [rn, e, qs.free, before], on="gpsimd")
            nk = k.tt(heads(ks.buf[:, :]), heads(rows.buf[:, QK:NQ]), bcast(sss.buf[:, c, DH:2 * DH], DK, DH), ALU.mult,
                      [rn, e, ks.free, before], on="gpsimd")
            nb = k.tt(heads(kbs.buf[:, :]), heads(ks.buf[:, :]), bcast(be.buf[:, :], DK, DH), ALU.mult,
                      [nk, b, kbs.free, before], on="gpsimd")
            rows.free = [nk]
            bvs, gts = bv.next(), gate.next()
            sgm = k.act(gts.buf[:, :], vg[:, HV:2 * HV], ACT.Sigmoid, [mv, gts.free, before])
            v = k.tt(bvs.buf[:, :].rearrange("p (h d) -> p h d", d=DV), vg[:, 0:HV].rearrange("p (h d) -> p h d", d=DV),
                     bcast(be.buf[:, :], DV, DH), ALU.mult, [sgm, b, bvs.free, before])
            be.free = [v, nb]
            g1 = k.tt(gts.buf[:, :], vg[:, HV:2 * HV], gts.buf[:, :], ALU.mult, [sgm])
            vg_bank.free = [v, g1]
            yield
            tb = turn_bank.buf
            t = k.transposes([(tb[:, n * P:(n + 1) * P], src, k.ident[:, :])
                              for n, src in enumerate((qs.buf[:, :], kbs.buf[:, :], ks.buf[:, :]))],
                             [nq, nk, nb, turn_bank.free])
            qs.free = kbs.free = [t]
            qt, kq = qkT.next(), kq_bd.next()
            e1 = k.act(qt.buf[:, :, :].rearrange("p a t -> p (a t)"), tb[:, 0:2 * P], after=[t, qt.free, before])
            e2 = k.tt(kq.buf[:, :, :], tb[:, 2 * P:3 * P].rearrange("p (o t) -> p o t", o=1).to_broadcast([P, DH, P]),
                      bcast(k.mask_quad[:, :], P, DH), ALU.mult, [e1, kq.free, before])
            turn_bank.free = [e1, e2]
            yield
            pb = prod_bank.buf
            mm = []
            for n in (1, 0):
                for b_ in range(B):
                    rows_ = slice(CH * b_, CH * (b_ + 1))
                    mm.append((pb[rows_, (1 - n) * P:(2 - n) * P], qt.buf[:, n, rows_], kq.buf[:, :, rows_], True, True))
            m = k.matmuls(mm, [e1, e2, prod_bank.free])
            kq.free = [m]
            at, tt_, ar = attn.next(), attnT.next(), a_rows.next()
            a = k.tt(ar.buf[:, :, :], pb[:, 0:P].rearrange("p (h s) -> p h s", h=DH),
                     k.mask_a[:, :].rearrange("p (o s) -> p o s", o=1).to_broadcast([P, DH, CH]), ALU.mult,
                     [m, ar.free, before])
            sent = p.dma("sync", io["systems"][ch // SOLVE % 2, ch % SOLVE].rearrange("h b t s -> (b t) h s"), ar.buf[:, :, :],
                         a_out[a_rows.at], [a, solved.get(ch // SOLVE - 2, {}).get("loaded")])
            ar.free = [sent]
            f = k.tt(at.buf[:, :, :], pb[:, P:2 * P].rearrange("p (h s) -> p h s", h=DH),
                     k.mask_attn[:, :].rearrange("p (o s) -> p o s", o=1).to_broadcast([P, DH, CH]), ALU.mult,
                     [m, at.free, before])
            prod_bank.free = [a, f]
            tr = p.step("vector", lambda e_: e_.transpose(tt_.buf[:, :, :].rearrange("p h s -> p (h s)"),
                                                          at.buf[:, :, :].rearrange("p h s -> p (h s)")),
                        [f, tt_.free, before])
            at.free = [tr]
            kept[ch] = dict(k=(ks, nk), qk=(qt, e1), attn=(tt_, tr), bv=(bvs, v), gate=(gts, g1), a=sent, h_read=mv,
                            qt_read=[m])
            yield

        def solve(n):
            chunks = range(n * SOLVE, (n + 1) * SOLVE)
            sa, iv, pr = sys_a.next(), inv.next(), prod.next()
            ld = p.dma("sync", sa.buf[:, :, :], io["systems"][n % 2].rearrange("c h b t s -> (c h b) t s"), a_in,
                       [[kept[c]["a"] for c in chunks], sa.free, before])
            solved[n] = dict(loaded=ld)
            z = k.memset(iv.buf[:, :, :], 0.0, on="gpsimd", after=[iv.free, before])
            flat = iv.buf[:, :, :].rearrange("p s t -> p (s t)")
            last = k.memset(flat[:, 0:CH * CH:CH + 1], 1.0, on="gpsimd", after=[z])
            yield
            for i in range(CH - 1):
                done, left = i + 1, CH - 1 - i
                row = iv.buf[:, 0:done, i:i + 1].to_broadcast([P, done, left])
                below = sa.buf[:, i + 1:CH, i].rearrange("p (o t) -> p o t", o=1).to_broadcast([P, done, left])
                m = k.tt(pr.buf[:, 0:done, 0:left], row, below, ALU.mult, [last, ld, pr.free, before])
                rows_ = iv.buf[:, 0:done, i + 1:CH]
                last = k.tt(rows_, rows_, pr.buf[:, 0:done, 0:left], ALU.add, [m])
                yield
            sa.free = [last]
            o = p.dma("sync", io["inverses"][n % 2].rearrange("c h b s t -> (c h b) s t"), iv.buf[:, :, :], inv_out,
                      [last, solved.get(n - 2, {}).get("read")])
            iv.free = [o]
            solved[n]["out"] = o

        def fetch(ch):
            s = invT.next()
            kpt = kept[ch]
            d = p.dma("sync", s.buf[:, :, :], io["inverses"][ch // SOLVE % 2, ch % SOLVE].rearrange("h b s t -> (b s) h t"),
                      inv_in[invT.at], [solved[ch // SOLVE]["out"], s.free, before])
            kpt["inv"] = (s, d)
            solved[ch // SOLVE]["read"] = d

        def on_diagonal(dst, src, after):
            return k.tt(dst.rearrange("p h (b t) -> p h b t", b=B),
                        src.rearrange("p h (o t) -> p h o t", o=1).to_broadcast([P, DH, B, CH]),
                        k.mask_quad[:, :].rearrange("p (o b u) -> p o b u", o=1, u=1).to_broadcast([P, DH, B, CH]),
                        ALU.mult, [after, before], on="gpsimd")

        def spread(ch):
            kpt = kept[ch]
            s, d = kpt["inv"]
            ib = inv_bd.next()
            done = on_diagonal(ib.buf[:, :, :], s.buf[:, :, :], [d, ib.free])
            s.free = [done]
            kpt["inv_bd"] = (ib, done)

        PAIRED = ("scalar", "vector", "vector", "scalar")
        s_written = [zeroed]
        updated = {}
        hold = {"u_free": [], "o": None}

        def scan(ch):
            kpt = kept[ch]
            (ks, nk), (qt, e1), (bvs, v), (tt_, tr) = kpt["k"], kpt["qk"], kpt["bv"], kpt["attn"]
            iv, iv_in = kpt["inv_bd"]
            cb, sb_, ob = chain_bank.buf, s_bank.buf, o_bank.buf
            rs = rhs.next()

            def by_batch(n, out, last):
                return [(out[CH * b_:CH * (b_ + 1), 0:HV], qt.buf[:, n, CH * b_:CH * (b_ + 1)],
                         s_bd[:, b_, :, :].rearrange("p h v -> p (h v)"), True, last) for b_ in range(B)]

            m = k.matmuls(by_batch(1, cb, True), [e1, s_written[0], chain_bank.free])
            if ch:
                evacuate(ch - 1)
                state["evacuated"] = ch
            d = k.tt(rs.buf[:, :], bvs.buf[:, :], cb[:, 0:HV], ALU.subtract, [m, v, rs.free, before])
            bvs.free = [d]
            yield
            m = k.matmuls([(cb[:, HV + h * DV:HV + (h + 1) * DV], iv.buf[:, h, :], rs.buf[:, h * DV:(h + 1) * DV],
                            True, True) for h in range(DH)], [d, iv_in])
            rs.free = [m]
            iv.free = [m]
            mq = k.matmuls(by_batch(0, ob, False), [o_bank.free], lint=False)
            u4 = cb[:, HV:2 * HV].rearrange("p (h v) -> p h v", h=DH)
            ub = [k.copy(u_bd[CH * b_:CH * (b_ + 1), :, b_, :], u4[CH * b_:CH * (b_ + 1), :, :],
                         [m, hold["u_free"], zeroed], on=eng) for b_, eng in enumerate(PAIRED)]
            chain_bank.free = ub
            yield
            m = k.matmuls([(sb_[DK * h:DK * (h + 1), 0:HV], ks.buf[:, h * DK:(h + 1) * DK],
                            u_bd[:, h, :, :].rearrange("p b v -> p (b v)"), ch == 0, ch == CHUNKS - 1) for h in range(DH)],
                          [ub, nk, s_bank.free], lint=False)
            ks.free = [m]
            s4 = sb_[:, 0:HV].rearrange("p (b v) -> p b v", b=B)
            sw = [k.copy(s_bd[DK * h:DK * (h + 1), :, h, :], s4[DK * h:DK * (h + 1), :, :], [m, mq, s_written[0]], on=eng)
                  for h, eng in enumerate(PAIRED)]
            s_written[0] = sw
            s_bank.free = sw
            mo = k.matmuls([(ob[CH * b_:CH * (b_ + 1), h * DV:(h + 1) * DV], tt_.buf[:, h, :], u_bd[:, h, b_, :], False, True)
                            for h in range(DH) for b_ in range(B)], [tr], lint=False)
            hold["u_free"] = [mo]
            tt_.free = [mo]
            qt.free = [mq] + kpt["qt_read"]
            kpt["o"] = mo
            yield

        def evacuate(ch):
            c = ch % TPG
            if c == 0:
                hold["rows"], hold["sums"], hold["read"] = on.next(), oss.next(), []
            ns, os_, o2, ob, mo = hold["rows"], hold["sums"], osq.next(), o_bank.buf, kept[ch]["o"]
            gts, g1 = kept[ch]["gate"]
            s = k.act(o2.buf[:, :], ob[:, 0:HV], ACT.Square, [mo, o2.free, before])
            e = k.tt(ns.buf[:, c, :], ob[:, 0:HV], gts.buf[:, :], ALU.mult, [s, g1, ns.free, before])
            o_bank.free = [e]
            gts.free = [e]
            r = k.reduce(os_.buf[:, c, :], o2.buf[:, :].rearrange("p (h v) -> p h v", h=DH), ALU.add,
                         after=[s, os_.free, before])
            o2.free = [r]
            hold["read"] += [e, r]

        def output(G):
            ns, os_, read = hold["rows"], hold["sums"], hold["read"]
            a = k.ts(os_.buf[:, :, :], os_.buf[:, :, :], 1.0 / DV, EPS, ALU.mult, ALU.add, after=[read], on="gpsimd")
            q = k.tt(os_.buf[:, :, :], os_.buf[:, :, :], k.half_power[:, 0:DH * TPG].rearrange("p (c h) -> p c h", c=TPG),
                     ALU.pow, [a], on="gpsimd")
            n = []
            for c in range(TPG):
                rows_ = ns.buf[:, c, :].rearrange("p (h v) -> p h v", h=DH)
                n.append(k.tt(rows_, rows_, bcast(os_.buf[:, c, :], DV, DH), ALU.mult, [q], on="gpsimd"))
                if c % 2:
                    yield
            os_.free = [n]
            ot, done = oT.next(), []
            for c in range(TPG):
                t = k.transposes([(turn_bank.buf[:, kt * P:(kt + 1) * P], ns.buf[:, c, kt * P:(kt + 1) * P], k.ident[:, :])
                                  for kt in range(KT)], [n[c], turn_bank.free])
                e = k.act(ot.buf[:, :, :, c, :], turn_bank.buf[:, 0:KT * P].rearrange("p (k b t) -> p k b t", k=KT, b=B),
                          after=[t, ot.free, before])
                turn_bank.free = [e]
                done.append(e)
                yield
            ns.free = [t]
            for b_ in range(B):
                bk = (prod_bank, qk_bank)[b_ % 2]
                m = k.matmuls([(bk.buf[:, 0:C], ot.buf[:, kt, b_, :, :].rearrange("p c t -> p (c t)"), w_o[:, kt, :],
                                kt == 0, kt == KT - 1) for kt in range(KT)], [done, bk.free, wo_scaled])
                x = k.xr[:, b_ * QB + G, :]
                a = k.tt(x, x, bk.buf[:, 0:C], ALU.add, [m])
                bk.free = [a]
                updated[b_ * QB + G] = a
                yield
            ot.free = [m]

        def run(gen):
            for _ in gen:
                pass

        def prepared(chunks):
            while state["prepared"] < chunks:
                next(prep)
                yield

        rounds = CHUNKS // SOLVE
        prep, outputs = prepare(), iter(())
        run(prepared(SOLVE))
        solving = solve(0)
        for _ in prepared(2 * SOLVE):
            next(solving, None)
        run(solving)
        for n in range(rounds):
            solving = None if n + 1 < rounds else iter(())
            chunks = list(range(n * SOLVE, (n + 1) * SOLVE))
            for ch in chunks[:3]:
                fetch(ch)
            spread(chunks[0])
            for i, ch in enumerate(chunks):
                if i + 3 < SOLVE:
                    fetch(ch + 3)
                if i + 1 < SOLVE:
                    spread(ch + 1)
                for j, _ in enumerate(scan(ch)):
                    if j == 0 and ch and ch % TPG == 0:
                        run(outputs)
                        outputs = output(ch // TPG - 1)
                    next(outputs, None)
                    next(prep, None)
                    if j != 1:
                        next(prep, None)
                    if solving is None and state["prepared"] >= (n + 2) * SOLVE:
                        solving = solve(n + 1)
                    if solving is not None:
                        for _ in range(2):
                            next(solving, None)
            run(solving)
            if n + 2 < rounds:
                for _ in prepared((n + 3) * SOLVE - 1):
                    next(outputs, None)
        run(outputs)
        evacuate(CHUNKS - 1)
        run(output(CHUNKS // TPG - 1))
        spare.free = prod.slots[0].free + [solved[rounds - 1]["out"]]
        k.xn.slots.append(spare)
        k.ready = updated


def store_residual(k):
    p, io = k.p, k.io
    for g in range(GROUPS):
        a = p.arrival(f"out{g}")
        p.dma("sync", io["out"][g * BANK:(g + 1) * BANK, :].rearrange("(i p) c -> p i c", p=P),
              k.xr[:, g * TPG:(g + 1) * TPG, :], a, [k.ready[i] for i in range(g * TPG, (g + 1) * TPG)])


STAGES = {"attention": attention, "ffn": ffn, "delta": delta}


def build(nc, io, stages=("attention", "ffn", "delta", "ffn")):
    with ExitStack() as ctx:
        k = Kernel(nc, ctx, io)
        allocate(k)
        load_constants(k)
        if stages[0] != "attention":
            load_x(k)
            load_ffn_weights(k)
        for n, s in enumerate(stages):
            STAGES[s](k)
        store_residual(k)
        k.p.run()




def constants():
    row, col = np.arange(P)[:, None], np.arange(P)[None, :]
    ch = np.arange(CH)[None, :]
    return np.concatenate([
        (row == col).astype(np.float32),
        np.where(col > row, np.float32(MASKED), np.float32(0)),
        np.where(ch < row % CH, np.float32(-1), np.float32(0)),
        (ch <= row % CH).astype(np.float32),
        (row // 32 == np.arange(4)[None, :]).astype(np.float32),
    ], axis=1)


def halves(w):
    return np.ascontiguousarray(w.reshape(KT, P, -1).transpose(1, 0, 2))


def lay_out(i):
    a = {n: np.asarray(v) for n, v in i.items()}
    A, D, F = "L0_attn_a_", "L0_attn_b_", "L0_ffn_"
    arrays = {
        "constants": constants(),
        "x": a[A + "x"].reshape(TOKENS, C),
        "wdqT": a[A + "W_dq"].T, "wuqT": a[A + "W_uq"].T, "wdkvT": a[A + "W_dkv"].T,
        "wuq": a[A + "W_uq"], "wuk": a[A + "W_uk"], "wdq": a[A + "W_dq"], "wuv": a[A + "W_uv"], "woT": a[A + "W_o"].T,
        "ffn_w": np.stack([halves(a[F + n].T) for n in ("wf", "wi", "wc", "wo", "uf", "ui", "uc", "uo")], axis=1),
        "ffn_b": np.stack([a[F + n].reshape(KT, P).T for n in ("bf", "bi", "bc", "in_c")], axis=1),
        "ffn_bo": a[F + "bo"].reshape(1, C),
        "d_qkb": halves(np.concatenate([a[D + "Wq"], a[D + "Wk"], a[D + "Wb"]], axis=1)),
        "d_vg": halves(np.concatenate([a[D + "Wv"], a[D + "Wg"]], axis=1)),
        "d_wo": halves(a[D + "Wo"]),
        "d_conv": halves(a[D + "conv_w"]),
        "d_norm": np.tile(a[D + "norm_w"], DH).reshape(KT, P).T,
    }
    return {n: np.ascontiguousarray(v) for n, v in arrays.items()}


def declare(nc, arrays):
    io = {n: nc.dram_tensor(f"in_{n}", v.shape, F32, kind="ExternalInput").ap() for n, v in arrays.items()}
    io["out"] = nc.dram_tensor("out_x", (TOKENS, C), F32, kind="ExternalOutput").ap()
    io["parts"] = nc.dram_tensor("qk_parts", (2, 3, C, TOKENS), BF16, kind="Internal").ap()
    io["systems"] = nc.dram_tensor("systems", (2, SOLVE, DH, B, CH, CH), F32, kind="Internal").ap()
    io["inverses"] = nc.dram_tensor("inverses", (2, SOLVE, DH, B, CH, CH), F32, kind="Internal").ap()
    return io


def kernel(**inputs):
    from concourse import bacc
    from concourse.bass_utils import run_bass_kernel_spmd

    arrays = lay_out(inputs)
    nc = bacc.Bacc("TRN2", target_bir_lowering=False, num_devices=1)
    io = declare(nc, arrays)
    build(nc, io)
    r = run_bass_kernel_spmd(nc, [{f"in_{n}": v for n, v in arrays.items()}], core_ids=[0])
    return r.results[0]["out_x"].reshape(B, T, C)
```
